# Optimizing a Trainium2 kernel written in Bass

```python
import numpy as np
import jax
import jax.numpy as jnp

def _softmax(x, axis=-1):
    return jax.nn.softmax(x, axis=axis)

def _gelu(x):
    return jax.nn.gelu(x, approximate=True)

def _silu(x):
    return jax.nn.silu(x)

def _sigmoid(x):
    return jax.nn.sigmoid(x)

def _layernorm(x, axis=-1, eps=1e-05):
    m = jnp.mean(x, axis=axis, keepdims=True)
    v = jnp.var(x, axis=axis, keepdims=True)
    return (x - m) / jnp.sqrt(v + eps)

def _scatter_add(tgt, idx, src, axis=0):
    return tgt.at[idx].add(src)

def _segment_sum(src, seg, n):
    return jax.ops.segment_sum(src, seg, n)
kernel_name = 'mk_flamingo_gated_d1_seqx_r4_6cda47'

def setup_inputs(seed: int=0):
    np.random.seed(seed)
    _w = jnp.asarray

    def _rec_inputs():
        import jax
        import jax.numpy as jnp
        _rk = jax.random.key(seed)
        x = 0.000341 + 1 * jax.random.normal(jax.random.fold_in(_rk, 1), (16, 256, 512), jnp.float32)
        _lenS = 256 - jax.random.randint(jax.random.fold_in(_rk, 7), (16,), 0, max(1, 256 // 4) + 1, jnp.int32)
        _lenS2 = 256 - jax.random.randint(jax.random.fold_in(_rk, 8), (16,), 0, max(1, 256 // 4) + 1, jnp.int32)
        _ctx_2048P = jax.random.normal(jax.random.fold_in(_rk, 11), (16, 16, 512), jnp.float32)
        _ctx_2048c = jax.random.dirichlet(jax.random.fold_in(_rk, 511), 0.3 * jnp.ones((16,), jnp.float32), (16, 256))
        _ctx_2048t = jnp.einsum('bsk,bkd->bsd', _ctx_2048c, _ctx_2048P)
        _ctx_2048t = _ctx_2048t * jax.lax.rsqrt(jnp.mean(jnp.square(_ctx_2048t)) + 1e-12) * 0.953939
        ctx_2048 = -1.47943e-05 + 1.00017 * (_ctx_2048t + 0.3 * jax.random.normal(jax.random.fold_in(_rk, 611), (16, 256, 512), jnp.float32))
        _g = jax.random.normal(jax.random.fold_in(_rk, 9001), (2, 1), jnp.float32)
        _g = jnp.sign(_g) * jnp.maximum(jnp.abs(_g), 1.0) + (_g == 0) * 1.0
        g_xattn = _g[0]
        g_ffn = _g[1]
        return (x, ctx_2048, g_xattn, g_ffn)
    x, ctx_2048, g_xattn, g_ffn = _rec_inputs()

    def _L0_xattn_setup():
        import jax, jax.numpy as jnp
        import numpy as np

        def _wkv(time_decay, time_first, k, v):
            w = -jnp.exp(time_decay)
            u = time_first
            B, T, C = k.shape
            aa = jnp.zeros((B, C), dtype=k.dtype)
            bb = jnp.zeros((B, C), dtype=k.dtype)
            pp = jnp.full((B, C), -1e+38, dtype=k.dtype)

            def step(carry, kv_t):
                aa, bb, pp = carry
                kt, vt = kv_t
                ww = u + kt
                q = jnp.maximum(pp, ww)
                e1 = jnp.exp(pp - q)
                e2 = jnp.exp(ww - q)
                y_t = (e1 * aa + e2 * vt) / (e1 * bb + e2)
                ww2 = pp + w
                q2 = jnp.maximum(ww2, kt)
                e1b = jnp.exp(ww2 - q2)
                e2b = jnp.exp(kt - q2)
                new_carry = (e1b * aa + e2b * vt, e1b * bb + e2b, q2)
                return (new_carry, y_t)
            ks = jnp.transpose(k, (1, 0, 2))
            vs = jnp.transpose(v, (1, 0, 2))
            _, ys = jax.lax.scan(step, (aa, bb, pp), (ks, vs))
            return jnp.transpose(ys, (1, 0, 2))
        key = jax.random.key(seed)
        k1, k2, k3, k4 = jax.random.split(key, 4)
        B, T, C = (8, 256, 512)
        return {'batch_size': B, 'seq_len': T, 'embedding_dim': C, 'time_decay': jax.random.normal(k1, (C,), dtype=jnp.float32), 'time_first': jax.random.normal(k2, (C,), dtype=jnp.float32), 'k': jax.random.normal(k3, (B, T, C), dtype=jnp.float32), 'v': jax.random.normal(k4, (B, T, C), dtype=jnp.float32)}
    _L0_xattn_all = _L0_xattn_setup()
    _L0_xattn_in = {k: v for k, v in _L0_xattn_all.items() if k in ('time_decay', 'time_first')}
    del _L0_xattn_all

    def _L0_ffn_setup():
        import jax, jax.numpy as jnp
        import numpy as np
        NUM_EXPERTS = 8
        TOP_K = 2
        IN_DIM = 512
        BOT_DIM = 128
        BATCH, SEQ = (4, 512)

        def _gelu(x):
            return jax.nn.gelu(x, approximate=False)
        key = jax.random.key(seed)
        ks = jax.random.split(key, 8)
        scale_d = 1.0 / np.sqrt(IN_DIM)
        scale_b = 1.0 / np.sqrt(BOT_DIM)
        return {'hidden_states': jax.random.normal(ks[0], (BATCH, SEQ, IN_DIM), jnp.float32), 'gate_w': jax.random.normal(ks[1], (NUM_EXPERTS, IN_DIM), jnp.float32) * scale_d, 'wd': jax.random.normal(ks[2], (NUM_EXPERTS, BOT_DIM, IN_DIM), jnp.float32) * scale_d, 'bd': jnp.zeros((NUM_EXPERTS, BOT_DIM), jnp.float32), 'wu': jax.random.normal(ks[3], (NUM_EXPERTS, IN_DIM, BOT_DIM), jnp.float32) * scale_b * 0.02, 'bu': jnp.zeros((NUM_EXPERTS, IN_DIM), jnp.float32), 'ws_d': jax.random.normal(ks[4], (BOT_DIM, IN_DIM), jnp.float32) * scale_d, 'bs_d': jnp.zeros((BOT_DIM,), jnp.float32), 'ws_u': jax.random.normal(ks[5], (IN_DIM, BOT_DIM), jnp.float32) * scale_b * 0.02, 'bs_u': jnp.zeros((IN_DIM,), jnp.float32)}
    _L0_ffn_all = _L0_ffn_setup()
    _L0_ffn_in = {k: v for k, v in _L0_ffn_all.items() if k in ('gate_w', 'wd', 'bd', 'wu', 'bu', 'ws_d', 'bs_d', 'ws_u', 'bs_u')}
    del _L0_ffn_all
    return {'x': x, 'ctx_2048': ctx_2048, 'g_xattn': g_xattn, 'g_ffn': g_ffn, 'L0_xattn_time_decay': _L0_xattn_in['time_decay'], 'L0_xattn_time_first': _L0_xattn_in['time_first'], 'L0_ffn_gate_w': _L0_ffn_in['gate_w'], 'L0_ffn_wd': _L0_ffn_in['wd'], 'L0_ffn_bd': _L0_ffn_in['bd'], 'L0_ffn_wu': _L0_ffn_in['wu'], 'L0_ffn_bu': _L0_ffn_in['bu'], 'L0_ffn_ws_d': _L0_ffn_in['ws_d'], 'L0_ffn_bs_d': _L0_ffn_in['bs_d'], 'L0_ffn_ws_u': _L0_ffn_in['ws_u'], 'L0_ffn_bs_u': _L0_ffn_in['bs_u']}

def reference(x, ctx_2048, g_xattn, g_ffn, L0_xattn_time_decay, L0_xattn_time_first, L0_ffn_gate_w, L0_ffn_wd, L0_ffn_bd, L0_ffn_wu, L0_ffn_bu, L0_ffn_ws_d, L0_ffn_bs_d, L0_ffn_ws_u, L0_ffn_bs_u):
    import jax
    import jax.numpy as jnp

    def _L0_xattn_ref(batch_size, seq_len, embedding_dim, time_decay, time_first, k, v):
        import jax, jax.numpy as jnp
        import numpy as np

        def _wkv(time_decay, time_first, k, v):
            w = -jnp.exp(time_decay)
            u = time_first
            B, T, C = k.shape
            aa = jnp.zeros((B, C), dtype=k.dtype)
            bb = jnp.zeros((B, C), dtype=k.dtype)
            pp = jnp.full((B, C), -1e+38, dtype=k.dtype)

            def step(carry, kv_t):
                aa, bb, pp = carry
                kt, vt = kv_t
                ww = u + kt
                q = jnp.maximum(pp, ww)
                e1 = jnp.exp(pp - q)
                e2 = jnp.exp(ww - q)
                y_t = (e1 * aa + e2 * vt) / (e1 * bb + e2)
                ww2 = pp + w
                q2 = jnp.maximum(ww2, kt)
                e1b = jnp.exp(ww2 - q2)
                e2b = jnp.exp(kt - q2)
                new_carry = (e1b * aa + e2b * vt, e1b * bb + e2b, q2)
                return (new_carry, y_t)
            ks = jnp.transpose(k, (1, 0, 2))
            vs = jnp.transpose(v, (1, 0, 2))
            _, ys = jax.lax.scan(step, (aa, bb, pp), (ks, vs))
            return jnp.transpose(ys, (1, 0, 2))
        assert seq_len <= 256
        return _wkv(time_decay, time_first, k, v)

    def _L0_ffn_ref(hidden_states, gate_w, wd, bd, wu, bu, ws_d, bs_d, ws_u, bs_u):
        import jax, jax.numpy as jnp
        import numpy as np
        NUM_EXPERTS = 8
        TOP_K = 2
        IN_DIM = 512
        BOT_DIM = 128
        BATCH, SEQ = (4, 512)

        def _gelu(x):
            return jax.nn.gelu(x, approximate=False)
        B, S, D = hidden_states.shape
        x = hidden_states.reshape(-1, D)
        T = x.shape[0]
        logits = x @ gate_w.T
        probs = jax.nn.softmax(logits.astype(jnp.float32), axis=-1)
        rw, sel = jax.lax.top_k(probs, TOP_K)
        rw = rw / rw.sum(axis=-1, keepdims=True)
        rw = rw.astype(x.dtype)
        combine = jnp.zeros((T, NUM_EXPERTS), x.dtype).at[jnp.arange(T)[:, None], sel].add(rw)
        down = jnp.einsum('td,ebd->teb', x, wd) + bd[None]
        h = _gelu(down) * combine[:, :, None]
        expert_out = jnp.einsum('teb,edb->td', h, wu) + combine @ bu
        shared = _gelu(x @ ws_d.T + bs_d) @ ws_u.T + bs_u
        out = (expert_out + shared).reshape(B, S, D)
        return out
    x = x + jnp.tanh(g_xattn[0]) * _L0_xattn_ref(16, 256, 512, L0_xattn_time_decay, L0_xattn_time_first, _layernorm(x, axis=-1), ctx_2048)
    x = x + jnp.tanh(g_ffn[0]) * _L0_ffn_ref(_layernorm(x, axis=-1), L0_ffn_gate_w, L0_ffn_wd, L0_ffn_bd, L0_ffn_wu, L0_ffn_bu, L0_ffn_ws_d, L0_ffn_bs_d, L0_ffn_ws_u, L0_ffn_bs_u)
    return x

_drawn_inputs = setup_inputs


def setup_inputs(seed=0):
    import zlib

    import numpy as np

    out = dict(_drawn_inputs(seed))
    spreads = {'L0_ffn_bd': (0.0, 0.8),
     'L0_ffn_bu': (0.0, 0.1),
     'L0_ffn_bs_d': (0.0, 0.8),
     'L0_ffn_bs_u': (0.0, 0.1)}
    factors = {'L0_ffn_wd': 7.959, 'L0_ffn_wu': 7.154, 'L0_ffn_ws_d': 5.896, 'L0_ffn_ws_u': 5.316}
    for name, (base, spread) in spreads.items():
        noise = np.random.default_rng([zlib.crc32(name.encode()), seed]).standard_normal(out[name].shape)
        drawn = base * np.exp(spread * noise) if base else spread * noise
        out[name] = jnp.asarray(drawn.astype(out[name].dtype))
    for name, factor in factors.items():
        out[name] = (out[name] * factor).astype(out[name].dtype)
    return out
```

```python
import numpy as np

import concourse.bass as bass
from concourse import mybir
from contextlib import ExitStack

B, T, C = 16, 256, 512
NE, BOT = 8, 128
P = 128
NH = NE + 1
GT = 512
SEQS = GT // T
NG = B * T // GT
NT = GT // P
NC = C // P
XS = 3
GATE = NC * NE
KB = 3 * NE + 3
SLOT = T + 1
EPS = 1e-5

O_ID = 0
O_BD = O_ID + P
O_TD = O_BD + NH
O_TF = O_TD + NC
O_GX = O_TF + NC
O_GF = O_GX + 1
O_IOTA = O_GF + 1
O_LOROW = O_IOTA + NE
O_HISIGN = O_LOROW + 1
O_SEL = O_HISIGN + 1
O_GW = O_SEL + NE
N_SMALL = O_GW + GATE

NW = NH * NC * BOT // C
RING = 4


def build(nc, x, ctx, smalls, bias_rows, w_down, w_up, out):
    F32, F32R, U32 = mybir.dt.float32, mybir.dt.float32r, mybir.dt.uint32
    ACT = mybir.ActivationFunctionType
    ALU = mybir.AluOpType

    x_d = x.rearrange("(g t p) c -> g t p c", t=NT, p=P)
    ctx_d = ctx.rearrange("(g t p) c -> g t p c", t=NT, p=P)
    out_d = out.rearrange("(g t p) c -> g t p c", t=NT, p=P)

    stack = ExitStack()
    with stack:
        def sb(name, shape, dt=F32):
            return stack.enter_context(nc.sbuf_tensor(name, shape, dt))

        def ps(name, shape):
            return stack.enter_context(nc.psum_tensor(name, shape, F32))

        def sem(name):
            return stack.enter_context(nc.semaphore(name))

        wd_hi = sb("wd_hi", [P, GATE + NH * NC * BOT], F32R)
        wd_lo = sb("wd_lo", [P, GATE + NH * NC * BOT], F32R)
        wu_hi = sb("wu_hi", [P, NH, C], F32R)
        wu_lo = sb("wu_lo", [P, NH, C], F32R)
        h_hi = sb("h_hi", [P, NH, GT], F32R)
        h_lo = sb("h_lo", [P, NH, GT], F32R)
        n_hi = sb("n_hi", [P, NC, GT], F32R)
        n_lo = sb("n_lo", [P, NC, GT], F32R)
        xs = sb("xs", [P, XS, NT, C])
        pk = sb("pk", [P, NT, C])
        cv = sb("cv", [P, NT, C])
        nd = sb("nd", [P, NC, 2, SEQS, SLOT])
        gl = sb("gl", [P, 2, GT])
        combT = sb("combT", [KB, GT], F32R)
        bias_r = sb("bias_r", [KB, C], F32R)
        sm = sb("sm", [P, N_SMALL])
        sel = sb("sel", [KB, NE], F32R)
        decay = sb("decay", [P, NC])
        s_old = sb("s_old", [P, NC])
        s_new = sb("s_new", [P, NC])
        tmp4 = sb("tmp4", [P, NC])
        tg = sb("tg", [P, 4])
        bn = sb("bn", [P, NT, 6])
        mv1 = sb("mv1", [P, NT, 2])
        ve1 = sb("ve1", [P, NT])
        rs1 = sb("rs1", [P, NT])
        nm1 = sb("nm1", [P, NT])
        bn2 = sb("bn2", [P, NT, 6])
        mv2 = sb("mv2", [P, NT, 2])
        ve2 = sb("ve2", [P, NT])
        rs2 = sb("rs2", [P, NT])
        nm2 = sb("nm2", [P, NT])
        mhalf = sb("mhalf", [P, NT])
        lg = sb("lg", [P, NT, NE])
        top = sb("top", [P, NT, 8])
        topi = sb("topi", [P, NT, 8], U32)
        gap = sb("gap", [P, NT])
        th = sb("th", [P, NT])
        wt = sb("wt", [P, 2, NT])
        oh = sb("oh", [P, 2, NT, NE])
        comb = sb("comb", [P, NT, KB], F32R)

        down_ps = ps("down_ps", [P, 2, GT])
        up_ps = ps("up_ps", [P, 2, C])
        work_ps = ps("work_ps", [P, 4, C])

        ident = sm[:, O_ID:O_ID + P]
        ident_k = sm[0:NE, O_ID:O_ID + NE]
        recip = cv
        bias_raw = xs[0:KB, 2, NT - 1, :]
        logit_sb = gl[0:NE, 1, :]

        def stage(n):
            return gl[:, 0, :] if n % RING == RING - 1 else xs[:, 2, n % RING, :]

        def down_at(i):
            return work_ps[:, 2, :] if i == NH - 1 else down_ps[:, i % 2, :]

        def normed(t):
            return nd[:, t, 1, :, 0:T]

        def normed_cols(t, c):
            s, at = c * P // T, c * P % T
            return nd[:, t, 1, s, at:at + P]

        def y_cols(c, t):
            s, at = t * P // T, t * P % T
            return nd[:, c, 0, s, at:at + P]

        def halves(ap):
            return ap.rearrange("p (s t) -> p s t", s=SEQS)

        small_in = sem("small_in")
        bias_in = sem("bias_in")
        w_in = [sem(f"w_in{n}") for n in range(RING)]
        x_in = [sem(f"x_in{t}") for t in range(NT)]
        ctx_in = [sem(f"ctx_in{t}") for t in range(NT)]
        slot_free = [sem(f"slot_free{t}") for t in range(NT)]
        w_hi = sem("w_hi")
        wd_split = sem("wd_split")
        wu_split = sem("wu_split")
        u_split = sem("u_split")
        tanh_done = sem("tanh_done")
        decay_step = sem("decay_step")
        scales_done = sem("scales_done")
        tg_done = sem("tg_done")
        const_step = sem("const_step")
        bn1_step = sem("bn1_step")
        ve1_done = sem("ve1_done")
        rs1_done = sem("rs1_done")
        nm1_done = sem("nm1_done")
        p_done = sem("p_done")
        pv_done = sem("pv_done")
        t_done = sem("t_done")
        sc_done = sem("sc_done")
        scan_done = sem("scan_done")
        nd_done = sem("nd_done")
        ln_done = sem("ln_done")
        r0_done = sem("r0_done")
        dr_done = sem("dr_done")
        r1_done = sem("r1_done")
        y_done = sem("y_done")
        yT_done = sem("yT_done")
        x1_done = sem("x1_done")
        bn2_step = sem("bn2_step")
        ve2_done = sem("ve2_done")
        rs2_done = sem("rs2_done")
        nm2_done = sem("nm2_done")
        hn_done = sem("hn_done")
        hT_done = sem("hT_done")
        n_hi_done = sem("n_hi_done")
        n_lo_done = sem("n_lo_done")
        logit_done = sem("logit_done")
        logit_out = sem("logit_out")
        lgT_done = sem("lgT_done")
        gate_step = sem("gate_step")
        th_done = sem("th_done")
        combT_ps = sem("combT_ps")
        combT_sb = sem("combT_sb")
        cb_done = sem("cb_done")
        down_done = sem("down_done")
        gelu_done = sem("gelu_done")
        mult_done = sem("mult_done")
        h_hi_done = sem("h_hi_done")
        h_lo_done = sem("h_lo_done")
        up_done = sem("up_done")
        fin_done = sem("fin_done")
        GS = 20
        CONSTS = 10

        block = stack.enter_context(nc.Block())

        def early(eng, value):
            if not isinstance(value, int):
                eng.compute_val(value)
            return value

        def over_groups(eng, body):
            with eng.Fori(0, NG // XS) as turn:
                for j in range(XS):
                    body(turn * XS + j, j, True, True)
            body(NG - 2, (NG - 2) % XS, True, False)
            body(NG - 1, (NG - 1) % XS, False, False)

        @block.sync
        def _(sp):
            def load_x(g, slot, t):
                sp.dma_start(xs[:, slot, t, :], x_d[g, t, :, :]).then_inc(x_in[t], 16)

            def load_ctx(g, t):
                sp.dma_start(cv[:, t, :], ctx_d[g, t, :, :]).then_inc(ctx_in[t], 16)

            def load_weights(n):
                if n >= RING:
                    m = n - RING
                    if m < NW:
                        sp.wait_ge(wd_split, m + 1)
                    else:
                        sp.wait_ge(wu_split, m - NW + 1)
                src = w_down[:, n * C:(n + 1) * C] if n < NW else w_up[:, (n - NW) * C:(n - NW + 1) * C]
                sp.dma_start(stage(n), src).then_inc(w_in[n % RING], 16)

            for t in range(NT):
                load_x(0, 0, t)
            sp.dma_start(sm[:, :], smalls).then_inc(small_in, 16)
            for t in range(NT):
                load_ctx(0, t)
            sp.dma_start(bias_raw, bias_rows).then_inc(bias_in, 16)
            for n in range(NW):
                load_weights(n)
            for t in range(NT):
                load_x(1, 1, t)
            for n in range(NW, 2 * NW):
                load_weights(n)
            for t in range(NT):
                sp.wait_ge(y_done, t + 1)
                load_ctx(1, t)
            sp.wait_ge(wu_split, NW)
            sp.wait_ge(const_step, CONSTS)
            for t in range(NT):
                sp.sem_inc(slot_free[t], 16)

            def body(g, slot, more, ahead):
                if ahead:
                    free, loaded = early(sp, g * 16 + 16), early(sp, g * 16 + 32)
                    for t in range(NT):
                        sp.wait_ge(slot_free[t], free)
                        sp.wait_ge(x_in[t], loaded)
                        load_x(g + 2, (slot + 2) % XS, t)
                    for t in range(NT):
                        sp.wait_ge(y_done, g * NC + NC + t + 1)
                        load_ctx(g + 2, t)
                for t in range(NT):
                    sp.wait_ge(fin_done, g * NT + t + 1)
                    sp.dma_start(out_d[g, t, :, :], xs[:, slot, t, :]).then_inc(slot_free[t], 16)

            over_groups(sp, body)
            for t in range(NT):
                sp.wait_ge(slot_free[t], NG * 16 + 16)

        @block.tensor
        def _(pe):
            def transpose_chunk(G, c, first=False):
                pe.wait_ge(p_done, G * NT + NT)
                pe.wait_ge(pv_done, G * NT + NT)
                if c < 2 and not first:
                    pe.wait_ge(n_hi_done, G * NT)
                    pe.wait_ge(n_lo_done, G * NT)
                    pe.wait_ge(gate_step, G * GS - GS + 5)
                if c >= 2:
                    pe.wait_ge(nd_done, G * NC + c - 1)
                pair = 2 * (c % 2)
                for s, src in enumerate((cv, pk)):
                    for t in range(NT):
                        last = nc.tensor.transpose(work_ps[:, pair + s, t * P:(t + 1) * P],
                                                   src[:, t, c * P:(c + 1) * P], ident)
                last.then_inc(t_done, 1)

            def transpose_y(G):
                pe.wait_ge(y_done, G * NC + NC)
                pe.wait_ge(gelu_done, G * NH)
                for t in range(NT):
                    for c in range(NC):
                        last = nc.tensor.transpose(work_ps[:, t, c * P:(c + 1) * P], y_cols(c, t), ident)
                    last.then_inc(yT_done, 1)

            def transpose_normed(G, pair):
                for t in (2 * pair, 2 * pair + 1):
                    pe.wait_ge(hn_done, G * NT + t + 1)
                    for c in range(NC):
                        last = nc.tensor.transpose(work_ps[:, t, c * P:(c + 1) * P], normed_cols(t, c), ident)
                    last.then_inc(hT_done, 1)

            def gate(G):
                pe.wait_ge(n_hi_done, G * NT + NT)
                pe.wait_ge(n_lo_done, G * NT + NT)
                k = 0
                for w, n in ((wd_hi, n_hi), (wd_hi, n_lo), (wd_lo, n_hi)):
                    for c in range(NC):
                        last = nc.tensor.matmul(work_ps[:, 3, :], w[:, c * NE:c * NE + P], n[:, c, :],
                                                start=(k == 0), stop=(k == 3 * NC - 1))
                        k += 1
                last.then_inc(logit_done, 1)

            def transpose_logits(G):
                copied = early(pe, G + 1)
                pe.wait_ge(small_in, 16)
                pe.wait_ge(logit_out, copied)
                for t in range(NT):
                    last = nc.tensor.transpose(work_ps[:, 3, t * NE:(t + 1) * NE],
                                               logit_sb[:, t * P:(t + 1) * P], ident_k)
                last.then_inc(lgT_done, 1)

            def down(g, i, more, between=None):
                if i == 0:
                    pe.wait_ge(n_hi_done, g * NT + NT)
                    pe.wait_ge(n_lo_done, g * NT + NT)
                if i == NH - 1:
                    if more:
                        pe.wait_ge(nd_done, g * NC + 2 * NC)
                elif i >= 2:
                    pe.wait_ge(gelu_done, g * NH + i - 1)
                k = 0
                for w, n in ((wd_hi, n_hi), (wd_hi, n_lo), (wd_lo, n_hi)):
                    for c in range(NC):
                        if k == 3 * NC // 2 and between:
                            between()
                        at = GATE + (i * NC + c) * BOT
                        last = nc.tensor.matmul(down_at(i), w[:, at:at + BOT], n[:, c, :],
                                                start=(k == 0), stop=(k == 3 * NC - 1))
                        k += 1
                last.then_inc(down_done, 1)

            def comb_transpose(g):
                pe.wait_ge(gate_step, g * GS + GS)
                for t in range(NT):
                    last = nc.tensor.transpose(up_ps[0:KB, 1, t * P:(t + 1) * P],
                                               comb[:, t, :].bitcast(F32), ident)
                last.then_inc(combT_ps, 1)

            def comb_spread(g, i):
                if i <= 2:
                    pe.wait_ge(combT_sb, g + 1)
                else:
                    pe.wait_ge(mult_done, g * NH + i - 1)
                nc.tensor.matmul(up_ps[:, (i + 1) % 2, :], sel[:, i - 1:i].to_broadcast([KB, P]), combT[:, :],
                                 start=True, stop=True).then_inc(cb_done, 1)

            def up(g, t, between={}):
                if t < 2:
                    pe.wait_ge(mult_done, g * NH + NH - 1 + t)
                else:
                    pe.wait_ge(fin_done, g * NT + t - 1)
                cols = slice(t * P, (t + 1) * P)
                nc.tensor.matmul(up_ps[:, t % 2, :], combT[:, cols], bias_r[:, :], start=True, stop=False)
                for i in range(NH):
                    if i in between:
                        between[i]()
                    if t == 0:
                        pe.wait_ge(h_hi_done, g * NH + i + 1)
                        pe.wait_ge(h_lo_done, g * NH + i + 1)
                    for k, (h, w) in enumerate(((h_hi, wu_hi), (h_hi, wu_lo), (h_lo, wu_hi))):
                        last = nc.tensor.matmul(up_ps[:, t % 2, :], h[:, i, cols], w[:, i, :],
                                                start=False, stop=(i == NH - 1 and k == 2))
                last.then_inc(up_done, 1)

            pe.wait_ge(small_in, 16)
            for c in range(NC):
                transpose_chunk(0, c, first=True)
            transpose_y(0)
            transpose_normed(0, 0)
            transpose_normed(0, 1)
            pe.wait_ge(wd_split, NW)
            pe.wait_ge(const_step, CONSTS)
            gate(0)

            def body(g, slot, more, ahead):
                down(g, 0, more, lambda: transpose_logits(g))
                if more:
                    transpose_chunk(g + 1, 0)
                down(g, 1, more, lambda: comb_transpose(g))
                comb_spread(g, 1)
                for i in range(2, NH):
                    if more and i in (2, 3, 5):
                        transpose_chunk(g + 1, {2: 1, 3: 2, 5: 3}[i])
                    down(g, i, more)
                    comb_spread(g, i)
                up(g, 0)
                up(g, 1)
                if more:
                    up(g, 2, {4: lambda: transpose_y(g + 1)})
                    up(g, 3, {4: lambda: transpose_normed(g + 1, 0), 8: lambda: transpose_normed(g + 1, 1)})
                    gate(g + 1)
                else:
                    up(g, 2)
                    up(g, 3)

            pe.wait_ge(wu_split, NW)
            over_groups(pe, body)

        @block.scalar
        def _(act):
            def exp_k(G, slot, t):
                act.wait_ge(nm1_done, G + 1)
                act.wait_ge(t_done, G * NC)
                nc.scalar.activation(pk[:, t, :], xs[:, slot, t, :], ACT.Exp, bias=nm1[:, t:t + 1],
                                     scale=rs1[:, t:t + 1]).then_inc(p_done, 1)

            def scan_copy(G, c):
                act.wait_ge(t_done, G * NC + c + 1)
                act.wait_ge(hT_done, G * NT)
                pair = 2 * (c % 2)
                nc.scalar.activation(nd[:, c, :, :, 1:SLOT],
                                     work_ps[:, pair:pair + 2, :].rearrange("p k (s t) -> p k s t", s=SEQS),
                                     ACT.Copy, scale=s_old[:, c:c + 1]).then_inc(sc_done, 1)

            def first_reciprocals(G):
                for c in range(NC):
                    act.wait_ge(nd_done, G * NC + c + 1)
                    act.wait_ge(t_done, G * NC + NC)
                    nc.scalar.activation(halves(recip[:, c, :]), nd[:, c, 1, :, 0:T], ACT.Ln).then_inc(ln_done, 1)
                for c in range(NC):
                    act.wait_ge(ln_done, G * NC + c + 1)
                    nc.scalar.activation(recip[:, c, :], recip[:, c, :], ACT.Exp, scale=-1.0).then_inc(r0_done, 1)

            def norm(G, slot, t):
                act.wait_ge(nm2_done, 2 * G + t // 2 + 1)
                act.wait_ge(y_done, G * NC + NC)
                nc.scalar.activation(normed(t), halves(xs[:, slot, t, :]), ACT.Identity, bias=nm2[:, t:t + 1],
                                     scale=rs2[:, t:t + 1]).then_inc(hn_done, 1)

            def norm_hi(G, t):
                act.wait_ge(hT_done, G * NT + t + 1)
                act.wait_ge(down_done, G * NH)
                cols = slice(t * P, (t + 1) * P)
                nc.scalar.activation(n_hi[:, :, cols], work_ps[:, t, :].rearrange("p (c n) -> p c n", c=NC), ACT.Copy).then_inc(n_hi_done, 1)

            def gate_act(G):
                act.wait_ge(logit_done, G + 1)
                nc.scalar.activation(logit_sb, work_ps[0:NE, 3, :], ACT.Copy).then_inc(logit_out, 1)
                act.wait_ge(gate_step, G * GS + 6)
                nc.scalar.activation(th[:, :], gap[:, :], ACT.Tanh, scale=0.5).then_inc(th_done, 1)

            def comb_copy(g):
                act.wait_ge(combT_ps, g + 1)
                nc.scalar.activation(combT[:, :], up_ps[0:KB, 1, :], ACT.Copy).then_inc(combT_sb, 1)

            def gelu(g, i):
                act.wait_ge(down_done, g * NH + i + 1)
                if i == 1:
                    act.wait_ge(lgT_done, g + 1)
                if i >= 2:
                    act.wait_ge(h_lo_done, g * NH + i - 1)
                nc.scalar.activation(gl[:, i % 2, :], down_at(i), ACT.Gelu,
                                     bias=sm[:, O_BD + i:O_BD + i + 1]).then_inc(gelu_done, 1)

            def block_hi(g, i):
                act.wait_ge(mult_done, g * NH + i + 1)
                nc.scalar.activation(h_hi[:, i, :], gl[:, i % 2, :], ACT.Copy).then_inc(h_hi_done, 1)

            def weight_hi(n):
                act.wait_ge(w_in[n % RING], 16 * (n // RING + 1))
                dst = wd_hi[:, GATE + n * C:GATE + (n + 1) * C] if n < NW else wu_hi[:, n - NW, :]
                nc.scalar.activation(dst, stage(n), ACT.Copy).then_inc(w_hi, 1)

            def second_half(G, slot):
                for t in range(NT):
                    norm(G, slot, t)
                for t in range(NT):
                    norm_hi(G, t)

            act.wait_ge(small_in, 16)
            nc.scalar.activation(th[:, 0:2], sm[:, O_GX:O_GX + 2], ACT.Tanh).then_inc(tanh_done, 1)
            nc.scalar.activation(tmp4[:, :], sm[:, O_TD:O_TD + NC], ACT.Exp).then_inc(decay_step, 1)
            act.wait_ge(decay_step, 1)
            nc.scalar.activation(decay[:, :], tmp4[:, :], ACT.Exp, scale=-1.0).then_inc(decay_step, 1)
            act.wait_ge(u_split, 2)
            nc.scalar.activation(s_old[:, :], s_old[:, :], ACT.Exp, scale=-1.0).then_inc(scales_done, 1)
            nc.scalar.activation(s_new[:, :], s_new[:, :], ACT.Exp).then_inc(scales_done, 1)
            for t in range(NT):
                exp_k(0, 0, t)
            act.wait_ge(scales_done, 2)
            for c in range(NC):
                scan_copy(0, c)
                weight_hi(c)
            first_reciprocals(0)
            for n in range(NC, NW):
                weight_hi(n)
            for t in range(NT):
                exp_k(1, 1, t)
            second_half(0, 0)
            for n in range(NW, 2 * NW):
                weight_hi(n)
            act.wait_ge(wu_split, NW)

            def body(g, slot, more, ahead):
                gate_act(g)
                gelu(g, 0)
                if more:
                    scan_copy(g + 1, 0)
                comb_copy(g)
                for i in range(1, NH):
                    gelu(g, i)
                    if more and i in (1, 2, 4):
                        scan_copy(g + 1, {1: 1, 2: 2, 4: 3}[i])
                    block_hi(g, i - 1)
                block_hi(g, NH - 1)
                if more:
                    first_reciprocals(g + 1)
                if ahead:
                    for t in range(NT):
                        exp_k(g + 2, (slot + 2) % XS, t)
                if more:
                    second_half(g + 1, (slot + 1) % XS)

            over_groups(act, body)

        @block.vector
        def _(dve):
            V = nc.vector

            def stats1(G, slot):
                for t in range(NT):
                    dve.wait_ge(x_in[t], G * 16 + 16)
                    V.bn_stats(bn[:, t, :], xs[:, slot, t, :]).then_inc(bn1_step, 1)
                measured = early(dve, G * 2 * NT + NT)
                dve.wait_ge(x_in[0], 16)
                dve.wait_ge(bn1_step, measured)
                for t in range(NT):
                    V.bn_aggr(mv1[:, t, :], bn[:, t, :]).then_inc(bn1_step, 1)
                dve.wait_ge(bn1_step, G * 2 * NT + 2 * NT)
                V.tensor_scalar(ve1[:, :], mv1[:, :, 1], EPS, None, ALU.add).then_inc(ve1_done, 1)

            def shift1(G):
                dve.wait_ge(rs1_done, G + 1)
                dve.wait_ge(p_done, G * NT)
                V.scalar_tensor_tensor(nm1[:, :], mv1[:, :, 0], -1.0, rs1[:, :], ALU.mult,
                                       ALU.mult).then_inc(nm1_done, 1)

            def scan(G, c):
                dve.wait_ge(sc_done, G * NC + c + 1)
                V.tensor_copy(nd[:, c, :, :, 0:1], nd[:, c, :, :, 1:2]).then_inc(scan_done, 1)
                dve.wait_ge(scan_done, G * 5 * NC + 5 * c + 1)
                for k in range(2):
                    for s in range(SEQS):
                        V.tensor_tensor_scan(nd[:, c, k, s, 1:SLOT], decay[:, c:c + 1].to_broadcast([P, T]),
                                             nd[:, c, k, s, 1:SLOT], 0.0, ALU.mult, ALU.add).then_inc(scan_done, 1)
                dve.wait_ge(scan_done, G * 5 * NC + 5 * (c + 1))
                pair = 2 * (c % 2)
                V.scalar_tensor_tensor(nd[:, c, :, :, 0:T],
                                       work_ps[:, pair:pair + 2, :].rearrange("p k (s t) -> p k s t", s=SEQS),
                                       s_new[:, c:c + 1], nd[:, c, :, :, 0:T], ALU.mult,
                                       ALU.add).then_inc(nd_done, 1)

            def quotient(G, c):
                dve.wait_ge(dr_done, G * NC + c + 1)
                V.scalar_tensor_tensor(halves(recip[:, c, :]), nd[:, c, 1, :, 0:T], 2.0, halves(recip[:, c, :]),
                                       ALU.subtract, ALU.mult).then_inc(r1_done, 1)
                dve.wait_ge(r1_done, G * NC + c + 1)
                V.tensor_tensor(nd[:, c, 0, :, 0:T], nd[:, c, 0, :, 0:T], halves(recip[:, c, :]),
                                ALU.mult).then_inc(y_done, 1)

            def residual(G, slot, pair):
                for t in (2 * pair, 2 * pair + 1):
                    dve.wait_ge(yT_done, G * NT + t + 1)
                    V.scalar_tensor_tensor(xs[:, slot, t, :], work_ps[:, t, :], tg[:, 0:1], xs[:, slot, t, :],
                                           ALU.mult, ALU.add).then_inc(x1_done, 1)

            def stats2(G, slot, pair):
                for t in (2 * pair, 2 * pair + 1):
                    dve.wait_ge(x1_done, G * NT + t + 1)
                    V.bn_stats(bn2[:, t, :], xs[:, slot, t, :]).then_inc(bn2_step, 1)
                measured = early(dve, G * 2 * NT + 4 * pair + 2)
                dve.wait_ge(x_in[0], 16)
                dve.wait_ge(bn2_step, measured)
                for t in (2 * pair, 2 * pair + 1):
                    V.bn_aggr(mv2[:, t, :], bn2[:, t, :]).then_inc(bn2_step, 1)
                dve.wait_ge(bn2_step, G * 2 * NT + 4 * pair + 4)
                at = slice(2 * pair, 2 * pair + 2)
                V.tensor_scalar(ve2[:, at], mv2[:, at, 1], EPS, None, ALU.add).then_inc(ve2_done, 1)

            def shift2(G, pair):
                dve.wait_ge(rs2_done, 2 * G + pair + 1)
                dve.wait_ge(hn_done, G * NT)
                at = slice(2 * pair, 2 * pair + 2)
                V.scalar_tensor_tensor(nm2[:, at], mv2[:, at, 0], -1.0, rs2[:, at], ALU.mult,
                                       ALU.mult).then_inc(nm2_done, 1)

            def norm_lo(G, t):
                dve.wait_ge(n_hi_done, G * NT + t + 1)
                cols = slice(t * P, (t + 1) * P)
                V.tensor_tensor(n_lo[:, :, cols], work_ps[:, t, :].rearrange("p (c n) -> p c n", c=NC), n_hi[:, :, cols].bitcast(F32),
                                ALU.subtract).then_inc(n_lo_done, 1)

            def routing(G):
                base = G * GS
                dve.wait_ge(lgT_done, G + 1)
                V.tensor_copy(lg[:, :, :], work_ps[:, 3, 0:NT * NE].rearrange("p (t e) -> p t e", t=NT)) \
                    .then_inc(gate_step, 1)
                for t in range(NT):
                    V.max(top[:, t, :], work_ps[:, 3, t * NE:(t + 1) * NE]).then_inc(gate_step, 1)
                dve.wait_ge(gate_step, base + 5)
                V.tensor_tensor(gap[:, :], top[:, :, 0], top[:, :, 1], ALU.subtract).then_inc(gate_step, 1)
                for t in range(NT):
                    V.max_index(topi[:, t, :], top[:, t, :], lg[:, t, :]).then_inc(gate_step, 1)
                dve.wait_ge(gate_step, base + 10)
                for k in range(2):
                    V.tensor_tensor(oh[:, k, :, :],
                                    sm[:, O_IOTA:O_IOTA + NE].unsqueeze(1).to_broadcast([P, NT, NE]),
                                    topi[:, :, k:k + 1].to_broadcast([P, NT, NE]), ALU.is_equal) \
                        .then_inc(gate_step, 1)
                dve.wait_ge(th_done, G + 1)
                V.tensor_scalar(wt[:, 0, :], th[:, :], tg[:, 2:3], tg[:, 2:3], ALU.mult, ALU.add) \
                    .then_inc(gate_step, 1)
                V.tensor_scalar(wt[:, 1, :], th[:, :], tg[:, 3:4], tg[:, 2:3], ALU.mult, ALU.add) \
                    .then_inc(gate_step, 1)
                dve.wait_ge(gate_step, base + 14)
                for k in range(2):
                    V.tensor_tensor(oh[:, k, :, :], oh[:, k, :, :],
                                    wt[:, k, :].unsqueeze(2).to_broadcast([P, NT, NE]), ALU.mult) \
                        .then_inc(gate_step, 1)
                dve.wait_ge(gate_step, base + 16)
                V.tensor_tensor(lg[:, :, :], oh[:, 0, :, :], oh[:, 1, :, :], ALU.add).then_inc(gate_step, 1)
                dve.wait_ge(gate_step, base + 17)
                dve.wait_ge(combT_ps, G)
                V.tensor_copy(comb[:, :, 0:NE], lg[:, :, :]).then_inc(gate_step, 1)
                V.tensor_copy(comb[:, :, 2 * NE:3 * NE], lg[:, :, :]).then_inc(gate_step, 1)
                dve.wait_ge(gate_step, base + 18)
                V.tensor_tensor(comb[:, :, NE:2 * NE], lg[:, :, :], comb[:, :, 0:NE].bitcast(F32),
                                ALU.subtract).then_inc(gate_step, 1)

            def mult(g, i):
                dve.wait_ge(gelu_done, g * NH + i + 1)
                if i == 0:
                    V.tensor_scalar(gl[:, 0, :], gl[:, 0, :], tg[:, 1:2], None, ALU.mult).then_inc(mult_done, 1)
                else:
                    dve.wait_ge(cb_done, g * NE + i)
                    V.tensor_tensor(gl[:, i % 2, :], up_ps[:, (i + 1) % 2, :], gl[:, i % 2, :],
                                    ALU.mult).then_inc(mult_done, 1)

            def finish(g, slot, t):
                dve.wait_ge(up_done, g * NT + t + 1)
                V.tensor_tensor(xs[:, slot, t, :], up_ps[:, t % 2, :], xs[:, slot, t, :],
                                ALU.add).then_inc(fin_done, 1)

            V.memset(mhalf[:, :], -0.5).then_inc(const_step, 1)
            stats1(0, 0)
            dve.wait_ge(small_in, 16)
            V.tensor_scalar(s_old[:, :], sm[:, O_TF:O_TF + NC], 0.0, None, ALU.max).then_inc(u_split, 1)
            V.tensor_scalar(s_new[:, :], sm[:, O_TF:O_TF + NC], 0.0, None, ALU.min).then_inc(u_split, 1)
            shift1(0)
            dve.wait_ge(tanh_done, 1)
            for k, (col, f) in enumerate(((0, -1.0), (1, 1.0), (1, 0.5), (1, -0.5))):
                V.tensor_scalar(tg[:, k:k + 1], th[:, col:col + 1], f, None, ALU.mult).then_inc(tg_done, 1)
            dve.wait_ge(tg_done, 4)
            for col in (3 * NE, 3 * NE + 2):
                V.tensor_copy(comb[:, :, col], tg[:, 1:2].to_broadcast([P, NT])).then_inc(const_step, 1)
            dve.wait_ge(const_step, 3)
            V.tensor_tensor(comb[:, :, 3 * NE + 1], tg[:, 1:2].to_broadcast([P, NT]),
                            comb[:, :, 3 * NE].bitcast(F32), ALU.subtract).then_inc(const_step, 1)
            V.tensor_copy(sel[:, :], sm[0:KB, O_SEL:O_SEL + NE]).then_inc(const_step, 1)
            V.tensor_copy(wd_hi[:, 0:GATE], sm[:, O_GW:O_GW + GATE]).then_inc(const_step, 1)
            dve.wait_ge(const_step, 6)
            V.tensor_tensor(wd_lo[:, 0:GATE], sm[:, O_GW:O_GW + GATE], wd_hi[:, 0:GATE].bitcast(F32),
                            ALU.subtract).then_inc(const_step, 1)
            dve.wait_ge(decay_step, 2)
            dve.wait_ge(scales_done, 2)
            for c in range(NC):
                scan(0, c)
            dve.wait_ge(bias_in, 16)
            V.tensor_copy(bias_r[:, :], bias_raw).then_inc(const_step, 1)
            dve.wait_ge(const_step, 8)
            V.tensor_scalar(bias_raw, bias_raw, sm[0:KB, O_LOROW:O_LOROW + 1], None, ALU.mult) \
                .then_inc(const_step, 1)
            dve.wait_ge(const_step, 9)
            V.scalar_tensor_tensor(bias_r[:, :], bias_r[:, :].bitcast(F32), sm[0:KB, O_HISIGN:O_HISIGN + 1],
                                   bias_raw, ALU.mult, ALU.add).then_inc(const_step, 1)
            for c in range(NC):
                quotient(0, c)
            stats1(1, 1)
            shift1(1)
            residual(0, 0, 0)
            stats2(0, 0, 0)
            residual(0, 0, 1)
            shift2(0, 0)
            stats2(0, 0, 1)
            shift2(0, 1)
            for t in range(NT):
                norm_lo(0, t)
            for n in range(NW):
                dve.wait_ge(w_hi, NW + n + 1)
                V.tensor_tensor(wu_lo[:, n, :], stage(NW + n), wu_hi[:, n, :].bitcast(F32),
                                ALU.subtract).then_inc(wu_split, 1)

            def body(g, slot, more, ahead):
                G, slot1 = g + 1, (slot + 1) % XS
                routing(g)
                mult(g, 0)
                for i in range(1, NH):
                    if more and i in (1, 2, 3, 5):
                        scan(G, {1: 0, 2: 1, 3: 2, 5: 3}[i])
                    mult(g, i)
                    if ahead and i == 3:
                        stats1(g + 2, (slot + 2) % XS)
                    if ahead and i == 5:
                        shift1(g + 2)
                finish(g, slot, 0)
                if more:
                    for c in range(NC):
                        quotient(G, c)
                    residual(G, slot1, 0)
                finish(g, slot, 1)
                if more:
                    stats2(G, slot1, 0)
                    residual(G, slot1, 1)
                    shift2(G, 0)
                    stats2(G, slot1, 1)
                    shift2(G, 1)
                finish(g, slot, 2)
                if more:
                    for t in range(NT):
                        norm_lo(G, t)
                finish(g, slot, 3)

            over_groups(dve, body)

        @block.gpsimd
        def _(pool):
            Q = nc.gpsimd

            def rstd1(G):
                pool.wait_ge(ve1_done, G + 1)
                pool.wait_ge(p_done, G * NT)
                Q.tensor_tensor(rs1[:, :], ve1[:, :], mhalf[:, :], ALU.pow).then_inc(rs1_done, 1)

            def rstd2(G, pair):
                pool.wait_ge(ve2_done, 2 * G + pair + 1)
                pool.wait_ge(hn_done, G * NT)
                at = slice(2 * pair, 2 * pair + 2)
                Q.tensor_tensor(rs2[:, at], ve2[:, at], mhalf[:, at], ALU.pow).then_inc(rs2_done, 1)

            def weigh_ctx(G, t):
                pool.wait_ge(p_done, G * NT + t + 1)
                pool.wait_ge(ctx_in[t], G * 16 + 16)
                Q.tensor_tensor(cv[:, t, :], cv[:, t, :], pk[:, t, :], ALU.mult).then_inc(pv_done, 1)

            def den_times_recip(G, c):
                pool.wait_ge(r0_done, G * NC + c + 1)
                Q.tensor_tensor(nd[:, c, 1, :, 0:T], nd[:, c, 1, :, 0:T], halves(recip[:, c, :]),
                                ALU.mult).then_inc(dr_done, 1)

            def block_lo(g, i):
                pool.wait_ge(h_hi_done, g * NH + i + 1)
                Q.tensor_tensor(h_lo[:, i, :], gl[:, i % 2, :], h_hi[:, i, :].bitcast(F32),
                                ALU.subtract).then_inc(h_lo_done, 1)

            def weight_lo(n):
                pool.wait_ge(w_hi, n + 1)
                at = slice(GATE + n * C, GATE + (n + 1) * C)
                Q.tensor_tensor(wd_lo[:, at], stage(n), wd_hi[:, at].bitcast(F32), ALU.subtract).then_inc(wd_split, 1)

            pool.wait_ge(const_step, 1)
            rstd1(0)
            for t in range(NT):
                weigh_ctx(0, t)
            for n in range(4):
                weight_lo(n)
            for c in range(NC):
                den_times_recip(0, c)
            for n in range(4, NW):
                weight_lo(n)
            rstd1(1)
            rstd2(0, 0)
            rstd2(0, 1)
            for t in range(NT):
                weigh_ctx(1, t)

            def body(g, slot, more, ahead):
                for i in range(NH):
                    block_lo(g, i)
                    if i == 4 and ahead:
                        rstd1(g + 2)
                if more:
                    for c in range(NC):
                        den_times_recip(g + 1, c)
                if more:
                    if ahead:
                        weigh_ctx(g + 2, 0)
                        weigh_ctx(g + 2, 1)
                    rstd2(g + 1, 0)
                    rstd2(g + 1, 1)
                    if ahead:
                        weigh_ctx(g + 2, 2)
                        weigh_ctx(g + 2, 3)

            over_groups(pool, body)


def kernel(x, ctx_2048, g_xattn, g_ffn, L0_xattn_time_decay, L0_xattn_time_first, L0_ffn_gate_w, L0_ffn_wd,
           L0_ffn_bd, L0_ffn_wu, L0_ffn_bu, L0_ffn_ws_d, L0_ffn_bs_d, L0_ffn_ws_u, L0_ffn_bs_u):
    import concourse.bacc as bacc
    from concourse.bass_utils import run_bass_kernel_spmd

    def a(v):
        return np.asarray(v)

    wd_all = np.concatenate([a(L0_ffn_ws_d)[None], a(L0_ffn_wd)])
    w_down = np.ascontiguousarray(wd_all.reshape(NH, BOT, NC, P).transpose(3, 0, 2, 1).reshape(P, NH * NC * BOT))
    wu_all = np.concatenate([a(L0_ffn_ws_u)[None], a(L0_ffn_wu)])
    w_up = np.ascontiguousarray(wu_all.transpose(2, 0, 1).reshape(P, NH * C))

    smalls = np.zeros((P, N_SMALL), np.float32)
    smalls[:, O_ID:O_ID + P] = np.eye(P, dtype=np.float32)
    smalls[:, O_BD:O_BD + NH] = np.concatenate([a(L0_ffn_bs_d)[None], a(L0_ffn_bd)]).T
    smalls[:, O_TD:O_TD + NC] = a(L0_xattn_time_decay).reshape(NC, P).T
    smalls[:, O_TF:O_TF + NC] = a(L0_xattn_time_first).reshape(NC, P).T
    smalls[:, O_GX:O_GX + 1] = a(g_xattn)
    smalls[:, O_GF:O_GF + 1] = a(g_ffn)
    smalls[:, O_IOTA:O_IOTA + NE] = np.arange(NE, dtype=np.float32)
    low = list(range(2 * NE, 3 * NE)) + [3 * NE + 2]
    smalls[low, O_LOROW] = 1.0
    smalls[:, O_HISIGN] = 1.0
    smalls[low, O_HISIGN] = -1.0
    for e in range(NE):
        smalls[[e, NE + e], O_SEL + e] = 1.0
    smalls[:, O_GW:O_GW + GATE] = a(L0_ffn_gate_w).reshape(NE, NC, P).transpose(2, 1, 0).reshape(P, GATE)
    bu, bs = a(L0_ffn_bu), a(L0_ffn_bs_u)[None]
    bias_rows = np.concatenate([bu, bu, bu, bs, bs, bs])

    nc = bacc.Bacc("TRN2", target_bir_lowering=False, num_devices=1)
    arrays = {"x": a(x).reshape(B * T, C), "ctx": a(ctx_2048).reshape(B * T, C), "smalls": smalls,
              "bias_rows": bias_rows, "w_down": w_down, "w_up": w_up}
    aps = [nc.dram_tensor(name, v.shape, mybir.dt.from_np(v.dtype), kind="ExternalInput").ap()
           for name, v in arrays.items()]
    out = nc.dram_tensor("out", (B * T, C), mybir.dt.float32, kind="ExternalOutput").ap()
    build(nc, *aps, out)
    r = run_bass_kernel_spmd(nc, [arrays], core_ids=[0])
    return r.results[0]["out"].reshape(B, T, C)
```

```python
import numpy as np

import concourse.bass as bass
from concourse import mybir
from contextlib import ExitStack

B, T, C = 16, 256, 512
NE, BOT = 8, 128
P = 128
NH = NE + 1
GT = 512
SEQS = GT // T
NG = B * T // GT
NT = GT // P
NC = C // P
XS = 3
GATE = 2 * NC * NE
KB = 3 * NE + 3
SLOT = T + 1
EPS = 1e-5
WARM = (12, 20, 12, 3, 8)

O_ID = 0
O_BD = O_ID + P
O_TD = O_BD + NH
O_TF = O_TD + NC
O_GX = O_TF + NC
O_GF = O_GX + 1
O_IOTA = O_GF + 1
O_LOROW = O_IOTA + NE
O_HISIGN = O_LOROW + 1
O_SEL = O_HISIGN + 1
O_GW = O_SEL + NE
N_SMALL = O_GW + NC * NE

NW = NH * NC * BOT // C
W_LOADS = 6
PER_LOAD = 2 * NW // W_LOADS


def build(nc, x, ctx, smalls, bias_rows, w_down, w_up, out):
    F32, F32R, U32 = mybir.dt.float32, mybir.dt.float32r, mybir.dt.uint32
    ACT = mybir.ActivationFunctionType
    ALU = mybir.AluOpType
    AX = mybir.AxisListType

    x_d = x.rearrange("(g t p) c -> g t p c", t=NT, p=P)
    ctx_d = ctx.rearrange("(g t p) c -> g t p c", t=NT, p=P)
    out_d = out.rearrange("(g t p) c -> g t p c", t=NT, p=P)

    stack = ExitStack()
    with stack:
        def sb(name, shape, dt=F32):
            return stack.enter_context(nc.sbuf_tensor(name, shape, dt))

        def ps(name, shape):
            return stack.enter_context(nc.psum_tensor(name, shape, F32))

        def sem(name):
            return stack.enter_context(nc.semaphore(name))

        with nc.sbuf_tensor("w_raw", [P, 2 * NW, C], F32) as w_raw:
            pass
        h_hi = sb("h_hi", [P, NH, GT], F32R)
        h_lo = sb("h_lo", [P, NH, GT], F32R)
        wd_hi = sb("wd_hi", [P, GATE + NH * NC * BOT], F32R)
        wd_lo = sb("wd_lo", [P, NH * NC * BOT], F32R)
        wu_hi = sb("wu_hi", [P, NH, C], F32R)
        wu_lo = sb("wu_lo", [P, NH, C], F32R)
        n_hi = sb("n_hi", [P, NC, GT], F32R)
        n_lo = sb("n_lo", [P, NC, GT], F32R)
        xs = sb("xs", [P, XS, NT, C])
        pk = sb("pk", [P, NT, C])
        cv = sb("cv", [P, NT, C])
        nd = sb("nd", [P, NC, 2, SEQS, SLOT])
        gl = sb("gl", [P, 2, GT])
        combT = sb("combT", [KB, GT], F32R)
        bias_r = sb("bias_r", [KB, C], F32R)
        sm = sb("sm", [P, N_SMALL])
        sel = sb("sel", [KB, NE], F32R)
        decay = sb("decay", [P, NC])
        s_old = sb("s_old", [P, NC])
        s_new = sb("s_new", [P, NC])
        tmp4 = sb("tmp4", [P, NC])
        tg = sb("tg", [P, 4])
        bn = sb("bn", [P, NT, 6])
        mv1 = sb("mv1", [P, NT, 2])
        ve1 = sb("ve1", [P, NT])
        rs1 = sb("rs1", [P, NT])
        nm1 = sb("nm1", [P, NT])
        bn2 = sb("bn2", [P, NT, 6])
        mv2 = sb("mv2", [P, NT, 2])
        ve2 = sb("ve2", [P, NT])
        rs2 = sb("rs2", [P, NT])
        nm2 = sb("nm2", [P, NT])
        mhalf = sb("mhalf", [P, NT])
        lg = sb("lg", [P, NT, NE])
        top = sb("top", [P, NT, 8])
        topi = sb("topi", [P, NT, 8], U32)
        gap = sb("gap", [P, NT])
        th = sb("th", [P, NT])
        wt = sb("wt", [P, 2, NT])
        oh = sb("oh", [P, 2, NT, NE])
        comb = sb("comb", [P, NT, KB], F32R)

        down_ps = ps("down_ps", [P, 2, GT])
        up_ps = ps("up_ps", [P, 2, C])
        work_ps = ps("work_ps", [P, 4, C])

        ident = sm[:, O_ID:O_ID + P]
        ident_k = sm[0:2 * NE, O_ID:O_ID + 2 * NE]
        recip = cv
        bias_raw = gl[0:KB, 0, :]
        logit_sb = gl[0:2 * NE, 1, :]

        def w_parts(n):
            if n < NW:
                return wd_hi[:, GATE + n * C:GATE + (n + 1) * C], wd_lo[:, n * C:(n + 1) * C]
            return wu_hi[:, n - NW, :], wu_lo[:, n - NW, :]

        def down_at(i):
            return work_ps[:, 2, :] if i == NH - 1 else down_ps[:, i % 2, :]

        def normed(t):
            return nd[:, t, 1, :, 0:T]

        def normed_cols(t, c):
            s, at = c * P // T, c * P % T
            return nd[:, t, 1, s, at:at + P]

        def y_cols(c, t):
            s, at = t * P // T, t * P % T
            return nd[:, c, 0, s, at:at + P]

        def halves(ap):
            return ap.rearrange("p (s t) -> p s t", s=SEQS)

        small_in = sem("small_in")
        bias_in = sem("bias_in")
        w_in = [sem(f"w_in{n}") for n in range(W_LOADS)]
        x_in = [sem(f"x_in{t}") for t in range(NT)]
        ctx_in = [sem(f"ctx_in{t}") for t in range(NT)]
        slot_free = [sem(f"slot_free{t}") for t in range(NT)]
        w_hi = sem("w_hi")
        w_split = sem("w_split")
        u_split = sem("u_split")
        tanh_done = sem("tanh_done")
        decay_step = sem("decay_step")
        scales_done = sem("scales_done")
        tg_done = sem("tg_done")
        const_step = sem("const_step")
        bn1_step = sem("bn1_step")
        ve1_done = sem("ve1_done")
        rs1_done = sem("rs1_done")
        nm1_done = sem("nm1_done")
        p_done = sem("p_done")
        pv_done = sem("pv_done")
        t_done = sem("t_done")
        sc_done = sem("sc_done")
        scan_done = sem("scan_done")
        nd_done = sem("nd_done")
        ln_done = sem("ln_done")
        r0_done = sem("r0_done")
        dr_done = sem("dr_done")
        r1_done = sem("r1_done")
        y_done = sem("y_done")
        yT_done = sem("yT_done")
        x1_done = sem("x1_done")
        bn2_step = sem("bn2_step")
        ve2_done = sem("ve2_done")
        rs2_done = sem("rs2_done")
        nm2_done = sem("nm2_done")
        hn_done = sem("hn_done")
        hT_done = sem("hT_done")
        n_hi_done = sem("n_hi_done")
        n_lo_done = sem("n_lo_done")
        logit_done = sem("logit_done")
        logit_out = sem("logit_out")
        lgT_done = sem("lgT_done")
        gate_step = sem("gate_step")
        th_done = sem("th_done")
        combT_ps = sem("combT_ps")
        combT_sb = sem("combT_sb")
        cb_done = sem("cb_done")
        down_done = sem("down_done")
        gelu_done = sem("gelu_done")
        mult_done = sem("mult_done")
        h_hi_done = sem("h_hi_done")
        h_lo_done = sem("h_lo_done")
        up_done = sem("up_done")
        fin_done = sem("fin_done")
        GS = 20
        CONSTS = 10

        block = stack.enter_context(nc.Block())

        def early(eng, value):
            if not isinstance(value, int):
                eng.compute_val(value)
            return value

        def over_groups(eng, body):
            with eng.Fori(0, NG // XS) as turn:
                for j in range(XS):
                    body(turn * XS + j, j, True, True)
            body(NG - 2, (NG - 2) % XS, True, False)
            body(NG - 1, (NG - 1) % XS, False, False)

        @block.sync
        def _(sp):
            def load_x(g, slot, t):
                sp.dma_start(xs[:, slot, t, :], x_d[g, t, :, :]).then_inc(x_in[t], 16)

            def load_ctx(g, t):
                sp.dma_start(cv[:, t, :], ctx_d[g, t, :, :]).then_inc(ctx_in[t], 16)

            def load_weights(n):
                w, first = (w_down, 0) if n < W_LOADS // 2 else (w_up, NW)
                at = slice(n * PER_LOAD, (n + 1) * PER_LOAD)
                sp.dma_start(w_raw[:, at, :], w[:, (at.start - first) * C:(at.stop - first) * C]
                             .rearrange("p (n c) -> p n c", c=C)).then_inc(w_in[n], 16)

            for t in range(NT):
                load_x(0, 0, t)
            sp.dma_start(sm[:, :], smalls).then_inc(small_in, 16)
            for t in range(NT):
                load_ctx(0, t)
            sp.dma_start(bias_raw, bias_rows).then_inc(bias_in, 16)
            for n in range(W_LOADS // 2):
                load_weights(n)
            for t in range(NT):
                sp.wait_ge(bn1_step, t + 1)
                load_x(1, 1, t)
            for n in range(W_LOADS // 2, W_LOADS):
                load_weights(n)
            for t in range(NT):
                sp.wait_ge(y_done, t + 1)
                load_ctx(1, t)
            for t in range(NT):
                sp.wait_ge(bn1_step, 2 * NT + t + 1)
                sp.sem_inc(slot_free[t], 16)

            def body(g, slot, more, ahead):
                if ahead:
                    free, loaded = early(sp, g * 16 + 16), early(sp, g * 16 + 32)
                    for t in range(NT):
                        sp.wait_ge(slot_free[t], free)
                        sp.wait_ge(x_in[t], loaded)
                        load_x(g + 2, (slot + 2) % XS, t)
                    for t in range(NT):
                        sp.wait_ge(y_done, g * NC + NC + t + 1)
                        load_ctx(g + 2, t)
                for t in range(NT):
                    sp.wait_ge(fin_done, g * NT + t + 1)
                    sp.dma_start(out_d[g, t, :, :], xs[:, slot, t, :]).then_inc(slot_free[t], 16)

            over_groups(sp, body)
            for t in range(NT):
                sp.wait_ge(slot_free[t], NG * 16 + 16)

        @block.tensor
        def _(pe):
            def transpose_chunk(G, c, first=False):
                pe.wait_ge(p_done, G * NT + NT)
                pe.wait_ge(pv_done, G * NT + NT)
                if c < 2 and not first:
                    pe.wait_ge(n_hi_done, G * NT)
                    pe.wait_ge(n_lo_done, G * NT)
                    pe.wait_ge(gate_step, G * GS - GS + 1)
                if c >= 2:
                    pe.wait_ge(nd_done, G * NC + c - 1)
                pair = 2 * (c % 2)
                for s, src in enumerate((cv, pk)):
                    for t in range(NT):
                        last = nc.tensor.transpose(work_ps[:, pair + s, t * P:(t + 1) * P],
                                                   src[:, t, c * P:(c + 1) * P], ident)
                last.then_inc(t_done, 1)

            def transpose_y(G):
                pe.wait_ge(y_done, G * NC + NC)
                pe.wait_ge(gelu_done, G * NH)
                for t in range(NT):
                    for c in range(NC):
                        last = nc.tensor.transpose(work_ps[:, t, c * P:(c + 1) * P], y_cols(c, t), ident)
                    last.then_inc(yT_done, 1)

            def transpose_normed(G, pair):
                for t in (2 * pair, 2 * pair + 1):
                    pe.wait_ge(hn_done, G * NT + t + 1)
                    for c in range(NC):
                        last = nc.tensor.transpose(work_ps[:, t, c * P:(c + 1) * P], normed_cols(t, c), ident)
                    last.then_inc(hT_done, 1)

            def gate(G):
                pe.wait_ge(n_hi_done, G * NT + NT)
                pe.wait_ge(n_lo_done, G * NT + NT)
                k = 0
                for c in range(NC):
                    for n in (n_hi, n_lo):
                        last = nc.tensor.matmul(work_ps[:, 3, :], wd_hi[:, c * 2 * NE:c * 2 * NE + P], n[:, c, :],
                                                start=(k == 0), stop=(k == 2 * NC - 1))
                        k += 1
                last.then_inc(logit_done, 1)

            def transpose_logits(G):
                copied = early(pe, G + 1)
                pe.wait_ge(small_in, 16)
                pe.wait_ge(logit_out, copied)
                for t in range(NT):
                    last = nc.tensor.transpose(work_ps[:, 3, 2 * t * NE:2 * (t + 1) * NE],
                                               logit_sb[:, t * P:(t + 1) * P], ident_k)
                last.then_inc(lgT_done, 1)

            def down(g, i, more, between=None):
                if i == 0:
                    pe.wait_ge(n_hi_done, g * NT + NT)
                    pe.wait_ge(n_lo_done, g * NT + NT)
                if i == NH - 1:
                    if more:
                        pe.wait_ge(nd_done, g * NC + 2 * NC)
                elif i >= 2:
                    pe.wait_ge(gelu_done, g * NH + i - 1)
                k = 0
                for c in range(NC):
                    if c == NC // 2 and between:
                        between()
                    at = (i * NC + c) * BOT
                    for w, at, n in ((wd_hi, GATE + at, n_hi), (wd_hi, GATE + at, n_lo), (wd_lo, at, n_hi)):
                        last = nc.tensor.matmul(down_at(i), w[:, at:at + BOT], n[:, c, :],
                                                start=(k == 0), stop=(k == 3 * NC - 1))
                        k += 1
                last.then_inc(down_done, 1)

            def comb_transpose(g):
                pe.wait_ge(gate_step, g * GS + GS)
                for t in range(NT):
                    last = nc.tensor.transpose(up_ps[0:KB, 1, t * P:(t + 1) * P],
                                               comb[:, t, :].bitcast(F32), ident)
                last.then_inc(combT_ps, 1)

            def comb_spread(g, i):
                if i <= 2:
                    pe.wait_ge(combT_sb, g + 1)
                else:
                    pe.wait_ge(mult_done, g * NH + i - 1)
                nc.tensor.matmul(up_ps[:, (i + 1) % 2, :], sel[:, i - 1:i].to_broadcast([KB, P]), combT[:, :],
                                 start=True, stop=True).then_inc(cb_done, 1)

            def up(g, t, between={}):
                if t == 0:
                    pe.wait_ge(w_split, 2 * NW)
                if t < 2:
                    pe.wait_ge(mult_done, g * NH + NH - 1 + t)
                else:
                    pe.wait_ge(fin_done, g * NT + t - 1)
                cols = slice(t * P, (t + 1) * P)
                nc.tensor.matmul(up_ps[:, t % 2, :], combT[:, cols], bias_r[:, :], start=True, stop=False)
                for i in range(NH):
                    if i in between:
                        between[i]()
                    if t == 0:
                        pe.wait_ge(h_hi_done, g * NH + i + 1)
                        pe.wait_ge(h_lo_done, g * NH + i + 1)
                    for k, (h, w) in enumerate(((h_hi, wu_hi), (h_hi, wu_lo), (h_lo, wu_hi))):
                        last = nc.tensor.matmul(up_ps[:, t % 2, :], h[:, i, cols], w[:, i, :],
                                                start=False, stop=(i == NH - 1 and k == 2))
                last.then_inc(up_done, 1)

            def keep_warm(n):
                for _ in range(n):
                    nc.tensor.matmul(down_ps[:, 0, :], wd_hi[:, GATE:GATE + P], wd_hi[:, GATE:GATE + C],
                                     start=True, stop=True)

            pe.wait_ge(small_in, 16)
            for _ in range(WARM[0]):
                nc.tensor.matmul(down_ps[:, 0, 0:P], ident, ident, start=True, stop=True)
            for c in range(NC):
                transpose_chunk(0, c, first=True)
            pe.wait_ge(w_hi, 1)
            pe.wait_ge(r0_done, 1)
            keep_warm(WARM[1])
            transpose_y(0)
            keep_warm(WARM[2])
            transpose_normed(0, 0)
            keep_warm(WARM[3])
            transpose_normed(0, 1)
            keep_warm(WARM[4])
            pe.wait_ge(w_split, NW)
            pe.wait_ge(const_step, CONSTS)
            gate(0)

            def body(g, slot, more, ahead):
                down(g, 0, more, lambda: transpose_logits(g))
                if more:
                    transpose_chunk(g + 1, 0)
                down(g, 1, more, lambda: comb_transpose(g))
                comb_spread(g, 1)
                for i in range(2, NH):
                    if more and i in (2, 3, 5):
                        transpose_chunk(g + 1, {2: 1, 3: 2, 5: 3}[i])
                    down(g, i, more)
                    comb_spread(g, i)
                up(g, 0)
                up(g, 1)
                if more:
                    up(g, 2, {4: lambda: transpose_y(g + 1)})
                    up(g, 3, {4: lambda: transpose_normed(g + 1, 0), 6: lambda: transpose_normed(g + 1, 1)})
                    gate(g + 1)
                else:
                    up(g, 2)
                    up(g, 3)

            over_groups(pe, body)

        @block.scalar
        def _(act):
            def exp_k(G, slot, t):
                act.wait_ge(nm1_done, G + 1)
                act.wait_ge(t_done, G * NC)
                nc.scalar.activation(pk[:, t, :], xs[:, slot, t, :], ACT.Exp, bias=nm1[:, t:t + 1],
                                     scale=rs1[:, t:t + 1]).then_inc(p_done, 1)

            def scan_copy(G, c):
                act.wait_ge(t_done, G * NC + c + 1)
                act.wait_ge(hT_done, G * NT)
                pair = 2 * (c % 2)
                nc.scalar.activation(nd[:, c, :, :, 1:SLOT],
                                     work_ps[:, pair:pair + 2, :].rearrange("p k (s t) -> p k s t", s=SEQS),
                                     ACT.Copy, scale=s_old[:, c:c + 1]).then_inc(sc_done, 1)

            def first_reciprocals(G):
                for c in range(NC):
                    act.wait_ge(nd_done, G * NC + c + 1)
                    act.wait_ge(t_done, G * NC + NC)
                    nc.scalar.activation(halves(recip[:, c, :]), nd[:, c, 1, :, 0:T], ACT.Ln).then_inc(ln_done, 1)
                for c in range(NC):
                    act.wait_ge(ln_done, G * NC + c + 1)
                    nc.scalar.activation(recip[:, c, :], recip[:, c, :], ACT.Exp, scale=-1.0).then_inc(r0_done, 1)

            def norm(G, slot, t):
                act.wait_ge(nm2_done, 2 * G + t // 2 + 1)
                act.wait_ge(y_done, G * NC + NC)
                nc.scalar.activation(normed(t), halves(xs[:, slot, t, :]), ACT.Identity, bias=nm2[:, t:t + 1],
                                     scale=rs2[:, t:t + 1]).then_inc(hn_done, 1)

            def norm_hi(G, t):
                act.wait_ge(hT_done, G * NT + t + 1)
                act.wait_ge(down_done, G * NH)
                cols = slice(t * P, (t + 1) * P)
                nc.scalar.activation(n_hi[:, :, cols], work_ps[:, t, :].rearrange("p (c n) -> p c n", c=NC), ACT.Copy).then_inc(n_hi_done, 1)

            def gate_act(G):
                act.wait_ge(logit_done, G + 1)
                nc.scalar.activation(logit_sb, work_ps[0:2 * NE, 3, :], ACT.Copy).then_inc(logit_out, 1)
                act.wait_ge(gate_step, G * GS + 6)
                nc.scalar.activation(th[:, :], gap[:, :], ACT.Tanh, scale=0.5).then_inc(th_done, 1)

            def comb_copy(g):
                act.wait_ge(combT_ps, g + 1)
                nc.scalar.activation(combT[:, :], up_ps[0:KB, 1, :], ACT.Copy).then_inc(combT_sb, 1)

            def gelu(g, i):
                act.wait_ge(down_done, g * NH + i + 1)
                if i == 1:
                    act.wait_ge(lgT_done, g + 1)
                if i >= 2:
                    act.wait_ge(h_lo_done, g * NH + i - 1)
                nc.scalar.activation(gl[:, i % 2, :], down_at(i), ACT.Gelu,
                                     bias=sm[:, O_BD + i:O_BD + i + 1]).then_inc(gelu_done, 1)

            def block_hi(g, i):
                act.wait_ge(w_split, 2 * NW)
                act.wait_ge(mult_done, g * NH + i + 1)
                nc.scalar.activation(h_hi[:, i, :], gl[:, i % 2, :], ACT.Copy).then_inc(h_hi_done, 1)

            def weight_hi(n):
                act.wait_ge(w_in[n // PER_LOAD], 16)
                hi, lo = w_parts(n)
                nc.scalar.activation(hi, w_raw[:, n, :], ACT.Copy).then_inc(w_hi, 1)

            def second_half(G, slot):
                for t in range(NT):
                    norm(G, slot, t)
                for t in range(NT):
                    norm_hi(G, t)

            act.wait_ge(small_in, 16)
            nc.scalar.activation(th[:, 0:2], sm[:, O_GX:O_GX + 2], ACT.Tanh).then_inc(tanh_done, 1)
            nc.scalar.activation(tmp4[:, :], sm[:, O_TD:O_TD + NC], ACT.Exp).then_inc(decay_step, 1)
            act.wait_ge(decay_step, 1)
            nc.scalar.activation(decay[:, :], tmp4[:, :], ACT.Exp, scale=-1.0).then_inc(decay_step, 1)
            act.wait_ge(u_split, 2)
            nc.scalar.activation(s_old[:, :], s_old[:, :], ACT.Exp, scale=-1.0).then_inc(scales_done, 1)
            nc.scalar.activation(s_new[:, :], s_new[:, :], ACT.Exp).then_inc(scales_done, 1)
            for t in range(NT):
                exp_k(0, 0, t)
            act.wait_ge(scales_done, 2)
            for n in range(3):
                weight_hi(n)
            scan_copy(0, 0)
            weight_hi(3)
            weight_hi(4)
            scan_copy(0, 1)
            weight_hi(5)
            scan_copy(0, 2)
            weight_hi(6)
            weight_hi(7)
            scan_copy(0, 3)
            first_reciprocals(0)
            for n in range(8, 2 * NW):
                weight_hi(n)
            second_half(0, 0)
            for t in range(NT):
                exp_k(1, 1, t)

            def body(g, slot, more, ahead):
                gate_act(g)
                gelu(g, 0)
                if more:
                    scan_copy(g + 1, 0)
                comb_copy(g)
                for i in range(1, NH):
                    gelu(g, i)
                    if more and i in (1, 2, 4):
                        scan_copy(g + 1, {1: 1, 2: 2, 4: 3}[i])
                    block_hi(g, i - 1)
                block_hi(g, NH - 1)
                if more:
                    first_reciprocals(g + 1)
                if ahead:
                    for t in range(NT):
                        exp_k(g + 2, (slot + 2) % XS, t)
                if more:
                    second_half(g + 1, (slot + 1) % XS)

            over_groups(act, body)

        @block.vector
        def _(dve):
            V = nc.vector

            def measure1(G, slot, tiles=range(NT)):
                for t in tiles:
                    dve.wait_ge(x_in[t], G * 16 + 16)
                    V.bn_stats(bn[:, t, :], xs[:, slot, t, :]).then_inc(bn1_step, 1)

            def stats1(G, slot, tiles=range(NT)):
                measure1(G, slot, tiles)
                measured = early(dve, G * 2 * NT + NT)
                dve.wait_ge(small_in, 16)
                dve.wait_ge(bn1_step, measured)
                for t in range(NT):
                    V.bn_aggr(mv1[:, t, :], bn[:, t, :]).then_inc(bn1_step, 1)
                dve.wait_ge(bn1_step, G * 2 * NT + 2 * NT)
                V.tensor_scalar(ve1[:, :], mv1[:, :, 1], EPS, None, ALU.add).then_inc(ve1_done, 1)

            def shift1(G):
                dve.wait_ge(rs1_done, G + 1)
                dve.wait_ge(p_done, G * NT)
                V.scalar_tensor_tensor(nm1[:, :], mv1[:, :, 0], -1.0, rs1[:, :], ALU.mult,
                                       ALU.mult).then_inc(nm1_done, 1)

            def scan(G, c):
                dve.wait_ge(sc_done, G * NC + c + 1)
                V.tensor_copy(nd[:, c, :, :, 0:1], nd[:, c, :, :, 1:2]).then_inc(scan_done, 1)
                dve.wait_ge(scan_done, G * 5 * NC + 5 * c + 1)
                for k in range(2):
                    for s in range(SEQS):
                        V.tensor_tensor_scan(nd[:, c, k, s, 1:SLOT], decay[:, c:c + 1].to_broadcast([P, T]),
                                             nd[:, c, k, s, 1:SLOT], 0.0, ALU.mult, ALU.add).then_inc(scan_done, 1)
                dve.wait_ge(scan_done, G * 5 * NC + 5 * (c + 1))
                pair = 2 * (c % 2)
                V.scalar_tensor_tensor(nd[:, c, :, :, 0:T],
                                       work_ps[:, pair:pair + 2, :].rearrange("p k (s t) -> p k s t", s=SEQS),
                                       s_new[:, c:c + 1], nd[:, c, :, :, 0:T], ALU.mult,
                                       ALU.add).then_inc(nd_done, 1)

            def quotient(G, c):
                dve.wait_ge(dr_done, G * NC + c + 1)
                V.scalar_tensor_tensor(halves(recip[:, c, :]), nd[:, c, 1, :, 0:T], 2.0, halves(recip[:, c, :]),
                                       ALU.subtract, ALU.mult).then_inc(r1_done, 1)
                dve.wait_ge(r1_done, G * NC + c + 1)
                V.tensor_tensor(nd[:, c, 0, :, 0:T], nd[:, c, 0, :, 0:T], halves(recip[:, c, :]),
                                ALU.mult).then_inc(y_done, 1)

            def residual(G, slot, pair):
                for t in (2 * pair, 2 * pair + 1):
                    dve.wait_ge(yT_done, G * NT + t + 1)
                    V.scalar_tensor_tensor(xs[:, slot, t, :], work_ps[:, t, :], tg[:, 0:1], xs[:, slot, t, :],
                                           ALU.mult, ALU.add).then_inc(x1_done, 1)

            def stats2(G, slot, pair):
                for t in (2 * pair, 2 * pair + 1):
                    dve.wait_ge(x1_done, G * NT + t + 1)
                    V.bn_stats(bn2[:, t, :], xs[:, slot, t, :]).then_inc(bn2_step, 1)
                measured = early(dve, G * 2 * NT + 4 * pair + 2)
                dve.wait_ge(small_in, 16)
                dve.wait_ge(bn2_step, measured)
                for t in (2 * pair, 2 * pair + 1):
                    V.bn_aggr(mv2[:, t, :], bn2[:, t, :]).then_inc(bn2_step, 1)
                dve.wait_ge(bn2_step, G * 2 * NT + 4 * pair + 4)
                at = slice(2 * pair, 2 * pair + 2)
                V.tensor_scalar(ve2[:, at], mv2[:, at, 1], EPS, None, ALU.add).then_inc(ve2_done, 1)

            def shift2(G, pair):
                dve.wait_ge(rs2_done, 2 * G + pair + 1)
                dve.wait_ge(hn_done, G * NT)
                at = slice(2 * pair, 2 * pair + 2)
                V.scalar_tensor_tensor(nm2[:, at], mv2[:, at, 0], -1.0, rs2[:, at], ALU.mult,
                                       ALU.mult).then_inc(nm2_done, 1)

            def norm_lo(G, t):
                dve.wait_ge(n_hi_done, G * NT + t + 1)
                cols = slice(t * P, (t + 1) * P)
                V.tensor_tensor(n_lo[:, :, cols], work_ps[:, t, :].rearrange("p (c n) -> p c n", c=NC), n_hi[:, :, cols].bitcast(F32),
                                ALU.subtract).then_inc(n_lo_done, 1)

            def routing(G):
                base = G * GS
                dve.wait_ge(lgT_done, G + 1)
                V.tensor_reduce(lg[:, :, :], work_ps[:, 3, 0:NT * 2 * NE]
                                .rearrange("p (t k e) -> p t e k", t=NT, k=2), AX.X, ALU.add).then_inc(gate_step, 1)
                summed = early(dve, base + 1)
                dve.wait_ge(small_in, 16)
                dve.wait_ge(gate_step, summed)
                for t in range(NT):
                    V.max(top[:, t, :], lg[:, t, :]).then_inc(gate_step, 1)
                dve.wait_ge(gate_step, base + 5)
                V.tensor_tensor(gap[:, :], top[:, :, 0], top[:, :, 1], ALU.subtract).then_inc(gate_step, 1)
                for t in range(NT):
                    V.max_index(topi[:, t, :], top[:, t, :], lg[:, t, :]).then_inc(gate_step, 1)
                dve.wait_ge(gate_step, base + 10)
                for k in range(2):
                    V.tensor_tensor(oh[:, k, :, :],
                                    sm[:, O_IOTA:O_IOTA + NE].unsqueeze(1).to_broadcast([P, NT, NE]),
                                    topi[:, :, k:k + 1].to_broadcast([P, NT, NE]), ALU.is_equal) \
                        .then_inc(gate_step, 1)
                dve.wait_ge(th_done, G + 1)
                V.tensor_scalar(wt[:, 0, :], th[:, :], tg[:, 2:3], tg[:, 2:3], ALU.mult, ALU.add) \
                    .then_inc(gate_step, 1)
                V.tensor_scalar(wt[:, 1, :], th[:, :], tg[:, 3:4], tg[:, 2:3], ALU.mult, ALU.add) \
                    .then_inc(gate_step, 1)
                dve.wait_ge(gate_step, base + 14)
                for k in range(2):
                    V.tensor_tensor(oh[:, k, :, :], oh[:, k, :, :],
                                    wt[:, k, :].unsqueeze(2).to_broadcast([P, NT, NE]), ALU.mult) \
                        .then_inc(gate_step, 1)
                dve.wait_ge(gate_step, base + 16)
                V.tensor_tensor(lg[:, :, :], oh[:, 0, :, :], oh[:, 1, :, :], ALU.add).then_inc(gate_step, 1)
                dve.wait_ge(gate_step, base + 17)
                dve.wait_ge(combT_ps, G)
                V.tensor_copy(comb[:, :, 0:NE], lg[:, :, :]).then_inc(gate_step, 1)
                V.tensor_copy(comb[:, :, 2 * NE:3 * NE], lg[:, :, :]).then_inc(gate_step, 1)
                dve.wait_ge(gate_step, base + 18)
                V.tensor_tensor(comb[:, :, NE:2 * NE], lg[:, :, :], comb[:, :, 0:NE].bitcast(F32),
                                ALU.subtract).then_inc(gate_step, 1)

            def mult(g, i):
                dve.wait_ge(gelu_done, g * NH + i + 1)
                if i == 0:
                    V.tensor_scalar(gl[:, 0, :], gl[:, 0, :], tg[:, 1:2], None, ALU.mult).then_inc(mult_done, 1)
                else:
                    dve.wait_ge(cb_done, g * NE + i)
                    V.tensor_tensor(gl[:, i % 2, :], up_ps[:, (i + 1) % 2, :], gl[:, i % 2, :],
                                    ALU.mult).then_inc(mult_done, 1)

            def finish(g, slot, t):
                dve.wait_ge(up_done, g * NT + t + 1)
                V.tensor_tensor(xs[:, slot, t, :], up_ps[:, t % 2, :], xs[:, slot, t, :],
                                ALU.add).then_inc(fin_done, 1)

            V.memset(mhalf[:, :], -0.5).then_inc(const_step, 1)
            stats1(0, 0)
            dve.wait_ge(small_in, 16)
            V.tensor_scalar(s_old[:, :], sm[:, O_TF:O_TF + NC], 0.0, None, ALU.max).then_inc(u_split, 1)
            V.tensor_scalar(s_new[:, :], sm[:, O_TF:O_TF + NC], 0.0, None, ALU.min).then_inc(u_split, 1)
            shift1(0)
            for t in range(NT):
                dve.wait_ge(p_done, t + 1)
                dve.wait_ge(ctx_in[t], 16)
                V.tensor_tensor(cv[:, t, :], cv[:, t, :], pk[:, t, :], ALU.mult).then_inc(pv_done, 1)
            dve.wait_ge(tanh_done, 1)
            for k, (col, f) in enumerate(((0, -1.0), (1, 1.0), (1, 0.5), (1, -0.5))):
                V.tensor_scalar(tg[:, k:k + 1], th[:, col:col + 1], f, None, ALU.mult).then_inc(tg_done, 1)
            dve.wait_ge(tg_done, 4)
            for col in (3 * NE, 3 * NE + 2):
                V.tensor_copy(comb[:, :, col], tg[:, 1:2].to_broadcast([P, NT])).then_inc(const_step, 1)
            dve.wait_ge(const_step, 3)
            V.tensor_tensor(comb[:, :, 3 * NE + 1], tg[:, 1:2].to_broadcast([P, NT]),
                            comb[:, :, 3 * NE].bitcast(F32), ALU.subtract).then_inc(const_step, 1)
            V.tensor_copy(sel[:, :], sm[0:KB, O_SEL:O_SEL + NE]).then_inc(const_step, 1)
            gate_w = sm[:, O_GW:O_GW + NC * NE].rearrange("p (c e) -> p c e", c=NC)
            gate_parts = wd_hi[:, 0:GATE].rearrange("p (c k e) -> p c k e", c=NC, k=2)
            V.tensor_copy(gate_parts[:, :, 0, :], gate_w).then_inc(const_step, 1)
            dve.wait_ge(const_step, 6)
            V.tensor_tensor(gate_parts[:, :, 1, :], gate_w, gate_parts[:, :, 0, :].bitcast(F32),
                            ALU.subtract).then_inc(const_step, 1)
            dve.wait_ge(bias_in, 16)
            V.tensor_copy(bias_r[:, :], bias_raw).then_inc(const_step, 1)
            dve.wait_ge(const_step, 8)
            V.tensor_scalar(bias_raw, bias_raw, sm[0:KB, O_LOROW:O_LOROW + 1], None, ALU.mult) \
                .then_inc(const_step, 1)
            dve.wait_ge(const_step, 9)
            V.scalar_tensor_tensor(bias_r[:, :], bias_r[:, :].bitcast(F32), sm[0:KB, O_HISIGN:O_HISIGN + 1],
                                   bias_raw, ALU.mult, ALU.add).then_inc(const_step, 1)
            dve.wait_ge(decay_step, 2)
            dve.wait_ge(scales_done, 2)
            for c in range(NC):
                scan(0, c)
            for c in range(NC):
                quotient(0, c)
            measure1(1, 1, range(NT // 2))
            residual(0, 0, 0)
            stats2(0, 0, 0)
            residual(0, 0, 1)
            shift2(0, 0)
            stats2(0, 0, 1)
            shift2(0, 1)
            stats1(1, 1, range(NT // 2, NT))
            for t in range(NT):
                norm_lo(0, t)
            shift1(1)
            for t in range(2):
                dve.wait_ge(p_done, NT + t + 1)
                dve.wait_ge(ctx_in[t], 32)
                V.tensor_tensor(cv[:, t, :], cv[:, t, :], pk[:, t, :], ALU.mult).then_inc(pv_done, 1)

            def body(g, slot, more, ahead):
                G, slot1 = g + 1, (slot + 1) % XS
                routing(g)
                mult(g, 0)
                for i in range(1, NH):
                    if more and i in (1, 2, 3, 5):
                        scan(G, {1: 0, 2: 1, 3: 2, 5: 3}[i])
                    mult(g, i)
                    if ahead and i == 3:
                        stats1(g + 2, (slot + 2) % XS)
                    if ahead and i == 5:
                        shift1(g + 2)
                finish(g, slot, 0)
                if more:
                    for c in range(NC):
                        quotient(G, c)
                    residual(G, slot1, 0)
                finish(g, slot, 1)
                if more:
                    stats2(G, slot1, 0)
                    residual(G, slot1, 1)
                    shift2(G, 0)
                    stats2(G, slot1, 1)
                    shift2(G, 1)
                finish(g, slot, 2)
                if more:
                    for t in range(NT):
                        norm_lo(G, t)
                finish(g, slot, 3)

            over_groups(dve, body)

        @block.gpsimd
        def _(pool):
            Q = nc.gpsimd

            def rstd1(G):
                pool.wait_ge(ve1_done, G + 1)
                pool.wait_ge(p_done, G * NT)
                Q.tensor_tensor(rs1[:, :], ve1[:, :], mhalf[:, :], ALU.pow).then_inc(rs1_done, 1)

            def rstd2(G, pair):
                pool.wait_ge(ve2_done, 2 * G + pair + 1)
                pool.wait_ge(hn_done, G * NT)
                at = slice(2 * pair, 2 * pair + 2)
                Q.tensor_tensor(rs2[:, at], ve2[:, at], mhalf[:, at], ALU.pow).then_inc(rs2_done, 1)

            def weigh_ctx(G, t):
                pool.wait_ge(p_done, G * NT + t + 1)
                pool.wait_ge(ctx_in[t], G * 16 + 16)
                Q.tensor_tensor(cv[:, t, :], cv[:, t, :], pk[:, t, :], ALU.mult).then_inc(pv_done, 1)

            def den_times_recip(G, c):
                pool.wait_ge(r0_done, G * NC + c + 1)
                Q.tensor_tensor(nd[:, c, 1, :, 0:T], nd[:, c, 1, :, 0:T], halves(recip[:, c, :]),
                                ALU.mult).then_inc(dr_done, 1)

            def block_lo(g, i):
                pool.wait_ge(h_hi_done, g * NH + i + 1)
                Q.tensor_tensor(h_lo[:, i, :], gl[:, i % 2, :], h_hi[:, i, :].bitcast(F32),
                                ALU.subtract).then_inc(h_lo_done, 1)

            def weight_lo(n):
                pool.wait_ge(w_hi, n + 1)
                hi, lo = w_parts(n)
                Q.tensor_tensor(lo, w_raw[:, n, :], hi.bitcast(F32), ALU.subtract).then_inc(w_split, 1)

            pool.wait_ge(const_step, 1)
            rstd1(0)
            for n in range(8):
                weight_lo(n)
            for c in range(NC):
                den_times_recip(0, c)
            for n in range(8, 2 * NW - 4):
                weight_lo(n)
            rstd2(0, 0)
            weight_lo(2 * NW - 4)
            weight_lo(2 * NW - 3)
            rstd2(0, 1)
            weight_lo(2 * NW - 2)
            rstd1(1)
            weight_lo(2 * NW - 1)
            weigh_ctx(1, 2)
            weigh_ctx(1, 3)

            def body(g, slot, more, ahead):
                for i in range(NH):
                    block_lo(g, i)
                    if i == 4 and ahead:
                        rstd1(g + 2)
                if more:
                    for c in range(NC):
                        den_times_recip(g + 1, c)
                if more:
                    if ahead:
                        weigh_ctx(g + 2, 0)
                        weigh_ctx(g + 2, 1)
                    rstd2(g + 1, 0)
                    rstd2(g + 1, 1)
                    if ahead:
                        weigh_ctx(g + 2, 2)
                        weigh_ctx(g + 2, 3)

            over_groups(pool, body)


def kernel(x, ctx_2048, g_xattn, g_ffn, L0_xattn_time_decay, L0_xattn_time_first, L0_ffn_gate_w, L0_ffn_wd,
           L0_ffn_bd, L0_ffn_wu, L0_ffn_bu, L0_ffn_ws_d, L0_ffn_bs_d, L0_ffn_ws_u, L0_ffn_bs_u):
    import concourse.bacc as bacc
    from concourse.bass_utils import run_bass_kernel_spmd

    def a(v):
        return np.asarray(v)

    wd_all = np.concatenate([a(L0_ffn_ws_d)[None], a(L0_ffn_wd)])
    w_down = np.ascontiguousarray(wd_all.reshape(NH, BOT, NC, P).transpose(3, 0, 2, 1).reshape(P, NH * NC * BOT))
    wu_all = np.concatenate([a(L0_ffn_ws_u)[None], a(L0_ffn_wu)])
    w_up = np.ascontiguousarray(wu_all.transpose(2, 0, 1).reshape(P, NH * C))

    smalls = np.zeros((P, N_SMALL), np.float32)
    smalls[:, O_ID:O_ID + P] = np.eye(P, dtype=np.float32)
    smalls[:, O_BD:O_BD + NH] = np.concatenate([a(L0_ffn_bs_d)[None], a(L0_ffn_bd)]).T
    smalls[:, O_TD:O_TD + NC] = a(L0_xattn_time_decay).reshape(NC, P).T
    smalls[:, O_TF:O_TF + NC] = a(L0_xattn_time_first).reshape(NC, P).T
    smalls[:, O_GX:O_GX + 1] = a(g_xattn)
    smalls[:, O_GF:O_GF + 1] = a(g_ffn)
    smalls[:, O_IOTA:O_IOTA + NE] = np.arange(NE, dtype=np.float32)
    low = list(range(2 * NE, 3 * NE)) + [3 * NE + 2]
    smalls[low, O_LOROW] = 1.0
    smalls[:, O_HISIGN] = 1.0
    smalls[low, O_HISIGN] = -1.0
    for e in range(NE):
        smalls[[e, NE + e], O_SEL + e] = 1.0
    smalls[:, O_GW:] = a(L0_ffn_gate_w).reshape(NE, NC, P).transpose(2, 1, 0).reshape(P, NC * NE)
    bu, bs = a(L0_ffn_bu), a(L0_ffn_bs_u)[None]
    bias_rows = np.concatenate([bu, bu, bu, bs, bs, bs])

    nc = bacc.Bacc("TRN2", target_bir_lowering=False, num_devices=1)
    arrays = {"x": a(x).reshape(B * T, C), "ctx": a(ctx_2048).reshape(B * T, C), "smalls": smalls,
              "bias_rows": bias_rows, "w_down": w_down, "w_up": w_up}
    aps = [nc.dram_tensor(name, v.shape, mybir.dt.from_np(v.dtype), kind="ExternalInput").ap()
           for name, v in arrays.items()]
    out = nc.dram_tensor("out", (B * T, C), mybir.dt.float32, kind="ExternalOutput").ap()
    build(nc, *aps, out)
    r = run_bass_kernel_spmd(nc, [arrays], core_ids=[0])
    return r.results[0]["out"].reshape(B, T, C)
```

```python
import numpy as np

import concourse.bass as bass
from concourse import mybir
from contextlib import ExitStack

B, T, C = 16, 256, 512
NE, BOT = 8, 128
P = 128
NH = NE + 1
GT = 512
SEQS = GT // T
NG = B * T // GT
NT = GT // P
NC = C // P
XS = 3
GATE = 2 * NC * NE
KB = 3 * NE + 3
SLOT = T + 1
EPS = 1e-5

O_ID = 0
O_BD = O_ID + P
O_TD = O_BD + NH
O_TF = O_TD + NC
O_GX = O_TF + NC
O_GF = O_GX + 1
O_IOTA = O_GF + 1
O_LOROW = O_IOTA + NE
O_HISIGN = O_LOROW + 1
O_SEL = O_HISIGN + 1
O_GW = O_SEL + NE
N_SMALL = O_GW + NC * NE

NW = NH * NC * BOT // C
W_LOADS = 6
PER_LOAD = 2 * NW // W_LOADS


def build(nc, x, ctx, smalls, bias_rows, w_down, w_up, out):
    F32, F32R, U32 = mybir.dt.float32, mybir.dt.float32r, mybir.dt.uint32
    ACT = mybir.ActivationFunctionType
    ALU = mybir.AluOpType
    AX = mybir.AxisListType

    x_d = x.rearrange("(g t p) c -> g t p c", t=NT, p=P)
    ctx_d = ctx.rearrange("(g t p) c -> g t p c", t=NT, p=P)
    out_d = out.rearrange("(g t p) c -> g t p c", t=NT, p=P)

    stack = ExitStack()
    with stack:
        def sb(name, shape, dt=F32):
            return stack.enter_context(nc.sbuf_tensor(name, shape, dt))

        def ps(name, shape):
            return stack.enter_context(nc.psum_tensor(name, shape, F32))

        def sem(name):
            return stack.enter_context(nc.semaphore(name))

        with nc.sbuf_tensor("w_raw", [P, 2 * NW, C], F32) as w_raw:
            pass
        h_hi = sb("h_hi", [P, NH, GT], F32R)
        h_lo = sb("h_lo", [P, NH, GT], F32R)
        wd_hi = sb("wd_hi", [P, GATE + NH * NC * BOT], F32R)
        wd_lo = sb("wd_lo", [P, NH * NC * BOT], F32R)
        wu_hi = sb("wu_hi", [P, NH, C], F32R)
        wu_lo = sb("wu_lo", [P, NH, C], F32R)
        n_hi = sb("n_hi", [P, NC, GT], F32R)
        n_lo = sb("n_lo", [P, NC, GT], F32R)
        xs = sb("xs", [P, XS, NT, C])
        pk = sb("pk", [P, NT, C])
        cv = sb("cv", [P, NT, C])
        nd = sb("nd", [P, NC, 2, SEQS, SLOT])
        gl = sb("gl", [P, 2, GT])
        combT = sb("combT", [KB, GT], F32R)
        bias_r = sb("bias_r", [KB, C], F32R)
        sm = sb("sm", [P, N_SMALL])
        sel = sb("sel", [KB, NE], F32R)
        decay = sb("decay", [P, NC])
        s_old = sb("s_old", [P, NC])
        s_new = sb("s_new", [P, NC])
        rate = sb("rate", [P, NC])
        tg = sb("tg", [P, 4])
        bn = sb("bn", [P, NT, 6])
        mv1 = sb("mv1", [P, NT, 2])
        ve1 = sb("ve1", [P, NT])
        rs1 = sb("rs1", [P, NT])
        nm1 = sb("nm1", [P, NT])
        bn2 = sb("bn2", [P, NT, 6])
        mv2 = sb("mv2", [P, NT, 2])
        ve2 = sb("ve2", [P, NT])
        rs2 = sb("rs2", [P, NT])
        nm2 = sb("nm2", [P, NT])
        mhalf = sb("mhalf", [P, NT])
        lg = sb("lg", [P, NT, NE])
        top = sb("top", [P, NT, 8])
        topi = sb("topi", [P, NT, 8], U32)
        gap = sb("gap", [P, NT])
        th = sb("th", [P, NT])
        wt = sb("wt", [P, 2, NT])
        oh = sb("oh", [P, 2, NT, NE])
        comb = sb("comb", [P, NT, KB], F32R)

        down_ps = ps("down_ps", [P, 2, GT])
        up_ps = ps("up_ps", [P, 2, C])
        work_ps = ps("work_ps", [P, 4, C])

        ident = sm[:, O_ID:O_ID + P]
        ident_k = sm[0:2 * NE, O_ID:O_ID + 2 * NE]
        recip = cv
        bias_raw = gl[0:KB, 0, :]
        logit_sb = gl[0:2 * NE, 1, :]

        def w_parts(n):
            if n < NW:
                return wd_hi[:, GATE + n * C:GATE + (n + 1) * C], wd_lo[:, n * C:(n + 1) * C]
            return wu_hi[:, n - NW, :], wu_lo[:, n - NW, :]

        def down_at(i):
            return work_ps[:, 2, :] if i == NH - 1 else down_ps[:, i % 2, :]

        def normed(t):
            return nd[:, t, 1, :, 0:T]

        def normed_cols(t, c):
            s, at = c * P // T, c * P % T
            return nd[:, t, 1, s, at:at + P]

        def y_cols(c, t):
            s, at = t * P // T, t * P % T
            return nd[:, c, 0, s, at:at + P]

        def halves(ap):
            return ap.rearrange("p (s t) -> p s t", s=SEQS)

        small_in = sem("small_in")
        bias_in = sem("bias_in")
        w_in = [sem(f"w_in{n}") for n in range(W_LOADS)]
        x_in = [sem(f"x_in{t}") for t in range(NT)]
        ctx_in = [sem(f"ctx_in{t}") for t in range(NT)]
        slot_free = [sem(f"slot_free{t}") for t in range(NT)]
        w_hi = sem("w_hi")
        w_split = sem("w_split")
        u_split = sem("u_split")
        tanh_done = sem("tanh_done")
        decay_step = sem("decay_step")
        scales_done = sem("scales_done")
        tg_done = sem("tg_done")
        const_step = sem("const_step")
        bn1_step = sem("bn1_step")
        ve1_done = sem("ve1_done")
        rs1_done = sem("rs1_done")
        nm1_done = sem("nm1_done")
        p_done = sem("p_done")
        pv_done = sem("pv_done")
        t_done = sem("t_done")
        sc_done = sem("sc_done")
        scan_done = sem("scan_done")
        nd_done = sem("nd_done")
        ln_done = sem("ln_done")
        r0_done = sem("r0_done")
        dr_done = sem("dr_done")
        r1_done = sem("r1_done")
        y_done = sem("y_done")
        yT_done = sem("yT_done")
        x1_done = sem("x1_done")
        bn2_step = sem("bn2_step")
        ve2_done = sem("ve2_done")
        rs2_done = sem("rs2_done")
        nm2_done = sem("nm2_done")
        hn_done = sem("hn_done")
        hT_done = sem("hT_done")
        n_hi_done = sem("n_hi_done")
        n_lo_done = sem("n_lo_done")
        logit_done = sem("logit_done")
        logit_out = sem("logit_out")
        lgT_done = sem("lgT_done")
        gate_step = sem("gate_step")
        th_done = sem("th_done")
        combT_ps = sem("combT_ps")
        combT_sb = sem("combT_sb")
        cb_done = sem("cb_done")
        down_done = sem("down_done")
        gelu_done = sem("gelu_done")
        mult_done = sem("mult_done")
        h_hi_done = sem("h_hi_done")
        h_lo_done = sem("h_lo_done")
        up_done = sem("up_done")
        fin_done = sem("fin_done")
        GS = 20
        CONSTS = 10

        LN_EXP, GELU_TANH = "natural_log_exp_and_others", "gelu_and_others"

        block = stack.enter_context(nc.Block())

        def early(eng, value):
            if not isinstance(value, int):
                eng.compute_val(value)
            return value

        def over_groups(eng, body):
            with eng.Fori(0, NG // XS) as turn:
                for j in range(XS):
                    body(turn * XS + j, j, True, True)
            body(NG - 2, (NG - 2) % XS, True, False)
            body(NG - 1, (NG - 1) % XS, False, False)

        @block.sync
        def _(sp):
            def load_x(g, slot, t):
                sp.dma_start(xs[:, slot, t, :], x_d[g, t, :, :]).then_inc(x_in[t], 16)

            def load_ctx(g, t):
                sp.dma_start(cv[:, t, :], ctx_d[g, t, :, :]).then_inc(ctx_in[t], 16)

            def load_weights(n):
                w, first = (w_down, 0) if n < W_LOADS // 2 else (w_up, NW)
                at = slice(n * PER_LOAD, (n + 1) * PER_LOAD)
                sp.dma_start(w_raw[:, at, :], w[:, (at.start - first) * C:(at.stop - first) * C]
                             .rearrange("p (n c) -> p n c", c=C)).then_inc(w_in[n], 16)

            def measured(G, t):
                return G * 2 * NT + 4 * (t // 2) + t % 2 + 1

            load_x(0, 0, 0)
            load_x(0, 0, 1)
            sp.dma_start(sm[:, :], smalls).then_inc(small_in, 16)
            load_x(0, 0, 2)
            load_x(0, 0, 3)
            for t in range(NT):
                load_ctx(0, t)
            sp.dma_start(bias_raw, bias_rows).then_inc(bias_in, 16)
            for n in range(W_LOADS // 2):
                load_weights(n)
            for t in range(NT):
                sp.wait_ge(bn1_step, measured(0, t))
                load_x(1, 1, t)
            for n in range(W_LOADS // 2, W_LOADS):
                load_weights(n)
            for t in range(NT):
                sp.wait_ge(y_done, t + 1)
                load_ctx(1, t)
            for t in range(NT):
                sp.wait_ge(bn1_step, measured(1, t))
                sp.sem_inc(slot_free[t], 16)

            def body(g, slot, more, ahead):
                if ahead:
                    free, loaded = early(sp, g * 16 + 16), early(sp, g * 16 + 32)
                    for t in range(NT):
                        sp.wait_ge(slot_free[t], free)
                        sp.wait_ge(x_in[t], loaded)
                        load_x(g + 2, (slot + 2) % XS, t)
                    for t in range(NT):
                        sp.wait_ge(y_done, g * NC + NC + t + 1)
                        load_ctx(g + 2, t)
                for t in range(NT):
                    sp.wait_ge(fin_done, g * NT + t + 1)
                    sp.dma_start(out_d[g, t, :, :], xs[:, slot, t, :]).then_inc(slot_free[t], 16)

            over_groups(sp, body)
            for t in range(NT):
                sp.wait_ge(slot_free[t], NG * 16 + 16)

        @block.tensor
        def _(pe):
            def transpose_chunk(G, c, first=False):
                if not (first and c == 0):
                    pe.wait_ge(p_done, G * NT + NT)
                    pe.wait_ge(pv_done, G * NT + NT)
                if c < 2 and not first:
                    pe.wait_ge(n_hi_done, G * NT)
                    pe.wait_ge(n_lo_done, G * NT)
                    pe.wait_ge(gate_step, G * GS - GS + 1)
                if c >= 2:
                    pe.wait_ge(nd_done, G * NC + c - 1)
                pair = 2 * (c % 2)
                for t in range(NT):
                    if first and c == 0:
                        pe.wait_ge(p_done, t + 1)
                        pe.wait_ge(pv_done, t + 1)
                    for s, src in enumerate((cv, pk)):
                        last = nc.tensor.transpose(work_ps[:, pair + s, t * P:(t + 1) * P],
                                                   src[:, t, c * P:(c + 1) * P], ident)
                last.then_inc(t_done, 1)

            def transpose_y(G):
                pe.wait_ge(y_done, G * NC + NC)
                pe.wait_ge(gelu_done, G * NH)
                for t in range(NT):
                    for c in range(NC):
                        last = nc.tensor.transpose(work_ps[:, t, c * P:(c + 1) * P], y_cols(c, t), ident)
                    last.then_inc(yT_done, 1)

            def transpose_normed(G, pair):
                for t in (2 * pair, 2 * pair + 1):
                    pe.wait_ge(hn_done, G * NT + t + 1)
                    for c in range(NC):
                        last = nc.tensor.transpose(work_ps[:, t, c * P:(c + 1) * P], normed_cols(t, c), ident)
                    last.then_inc(hT_done, 1)

            def gate(G):
                for part, (n, done) in enumerate(((n_hi, n_hi_done), (n_lo, n_lo_done))):
                    pe.wait_ge(done, G * NT + NT)
                    for c in range(NC):
                        last = nc.tensor.matmul(down_ps[:, 1, :], wd_hi[:, c * 2 * NE:c * 2 * NE + P], n[:, c, :],
                                                start=(part == 0 and c == 0), stop=(part == 1 and c == NC - 1))
                last.then_inc(logit_done, 1)

            def transpose_logits(G):
                copied = early(pe, G + 1)
                pe.wait_ge(small_in, 16)
                pe.wait_ge(logit_out, copied)
                for t in range(NT):
                    last = nc.tensor.transpose(work_ps[:, 3, 2 * t * NE:2 * (t + 1) * NE],
                                               logit_sb[:, t * P:(t + 1) * P], ident_k)
                last.then_inc(lgT_done, 1)

            def down(g, i, more, between=None):
                if i == 0:
                    pe.wait_ge(n_hi_done, g * NT + NT)
                    pe.wait_ge(n_lo_done, g * NT + NT)
                if i == NH - 1:
                    if more:
                        pe.wait_ge(nd_done, g * NC + 2 * NC)
                elif i >= 2:
                    pe.wait_ge(gelu_done, g * NH + i - 1)
                k = 0
                for c in range(NC):
                    if c == NC // 2 and between:
                        between()
                    at = (i * NC + c) * BOT
                    for w, at, n in ((wd_hi, GATE + at, n_hi), (wd_hi, GATE + at, n_lo), (wd_lo, at, n_hi)):
                        last = nc.tensor.matmul(down_at(i), w[:, at:at + BOT], n[:, c, :],
                                                start=(k == 0), stop=(k == 3 * NC - 1))
                        k += 1
                last.then_inc(down_done, 1)

            def comb_transpose(g):
                pe.wait_ge(gate_step, g * GS + GS)
                for t in range(NT):
                    last = nc.tensor.transpose(up_ps[0:KB, 1, t * P:(t + 1) * P],
                                               comb[:, t, :].bitcast(F32), ident)
                last.then_inc(combT_ps, 1)

            def comb_spread(g, i):
                if i <= 2:
                    pe.wait_ge(combT_sb, g + 1)
                else:
                    pe.wait_ge(mult_done, g * NH + i - 1)
                nc.tensor.matmul(up_ps[:, (i + 1) % 2, :], sel[:, i - 1:i].to_broadcast([KB, P]), combT[:, :],
                                 start=True, stop=True).then_inc(cb_done, 1)

            def up(g, t, between=()):
                if t == 0:
                    pe.wait_ge(w_split, 2 * NW)
                    pe.wait_ge(const_step, CONSTS)
                if t < 2:
                    pe.wait_ge(mult_done, g * NH + NH - 1 + t)
                else:
                    pe.wait_ge(fin_done, g * NT + t - 1)
                cols = slice(t * P, (t + 1) * P)
                nc.tensor.matmul(up_ps[:, t % 2, :], combT[:, cols], bias_r[:, :], start=True, stop=False)
                for i in range(NH):
                    if i in between:
                        between[i]()
                    if t == 0:
                        pe.wait_ge(h_hi_done, g * NH + i + 1)
                        pe.wait_ge(h_lo_done, g * NH + i + 1)
                    for k, (h, w) in enumerate(((h_hi, wu_hi), (h_hi, wu_lo), (h_lo, wu_hi))):
                        last = nc.tensor.matmul(up_ps[:, t % 2, :], h[:, i, cols], w[:, i, :],
                                                start=False, stop=(i == NH - 1 and k == 2))
                last.then_inc(up_done, 1)

            def keep_warm(n):
                for _ in range(n):
                    nc.tensor.matmul(down_ps[:, 0, :], wd_hi[:, GATE:GATE + P], wd_hi[:, GATE:GATE + C],
                                     start=True, stop=True)

            pe.wait_ge(small_in, 16)
            for _ in range(10):
                nc.tensor.matmul(down_ps[:, 0, 0:P], ident, ident, start=True, stop=True)
            transpose_chunk(0, 0, first=True)
            transpose_chunk(0, 1, first=True)
            pe.wait_ge(w_hi, 1)
            keep_warm(7)
            transpose_chunk(0, 2, first=True)
            keep_warm(6)
            transpose_chunk(0, 3, first=True)
            pe.wait_ge(r0_done, 1)
            keep_warm(20)
            transpose_y(0)
            keep_warm(17)
            transpose_normed(0, 0)
            keep_warm(7)
            transpose_normed(0, 1)
            keep_warm(5)
            pe.wait_ge(w_split, NW)
            pe.wait_ge(const_step, CONSTS - 3)
            gate(0)

            def body(g, slot, more, ahead):
                down(g, 0, more, lambda: transpose_logits(g))
                if more:
                    transpose_chunk(g + 1, 0)
                down(g, 1, more, lambda: comb_transpose(g))
                comb_spread(g, 1)
                for i in range(2, NH):
                    if more and i in (2, 3, 5):
                        transpose_chunk(g + 1, {2: 1, 3: 2, 5: 3}[i])
                    down(g, i, more)
                    comb_spread(g, i)
                up(g, 0)
                up(g, 1)
                if more:
                    up(g, 2, {2: lambda: transpose_y(g + 1)})
                    up(g, 3, {3: lambda: transpose_normed(g + 1, 0), 5: lambda: transpose_normed(g + 1, 1)})
                    gate(g + 1)
                else:
                    up(g, 2)
                    up(g, 3)

            over_groups(pe, body)

        @block.scalar
        def _(act):
            def exp_k(G, slot, t):
                act.wait_ge(nm1_done, 2 * G + t // 2 + 1)
                act.wait_ge(t_done, G * NC)
                nc.scalar.activation(pk[:, t, :], xs[:, slot, t, :], ACT.Exp, bias=nm1[:, t:t + 1],
                                     scale=rs1[:, t:t + 1]).then_inc(p_done, 1)

            def scan_copy(G, c):
                act.wait_ge(t_done, G * NC + c + 1)
                act.wait_ge(hT_done, G * NT)
                pair = 2 * (c % 2)
                nc.scalar.activation(nd[:, c, :, :, 1:SLOT],
                                     work_ps[:, pair:pair + 2, :].rearrange("p k (s t) -> p k s t", s=SEQS),
                                     ACT.Copy, scale=s_old[:, c:c + 1]).then_inc(sc_done, 1)

            def first_reciprocals(G, chunks):
                for c in chunks:
                    act.wait_ge(nd_done, G * NC + c + 1)
                    act.wait_ge(t_done, G * NC + NC)
                    nc.scalar.activation(halves(recip[:, c, :]), nd[:, c, 1, :, 0:T], ACT.Ln).then_inc(ln_done, 1)
                for c in chunks:
                    act.wait_ge(ln_done, G * NC + c + 1)
                    nc.scalar.activation(recip[:, c, :], recip[:, c, :], ACT.Exp, scale=-1.0).then_inc(r0_done, 1)

            def norm(G, slot, t):
                act.wait_ge(nm2_done, 2 * G + t // 2 + 1)
                act.wait_ge(y_done, G * NC + NC)
                nc.scalar.activation(normed(t), halves(xs[:, slot, t, :]), ACT.Identity, bias=nm2[:, t:t + 1],
                                     scale=rs2[:, t:t + 1]).then_inc(hn_done, 1)

            def norm_hi(G, t):
                act.wait_ge(hT_done, G * NT + t + 1)
                act.wait_ge(down_done, G * NH)
                cols = slice(t * P, (t + 1) * P)
                nc.scalar.activation(n_hi[:, :, cols], work_ps[:, t, :].rearrange("p (c n) -> p c n", c=NC),
                                     ACT.Copy).then_inc(n_hi_done, 1)

            def gate_act(G):
                act.wait_ge(logit_done, G + 1)
                nc.scalar.activation(logit_sb, down_ps[0:2 * NE, 1, :], ACT.Copy).then_inc(logit_out, 1)
                nc.scalar.preload_act_table_set(GELU_TANH)
                act.wait_ge(gate_step, G * GS + 6)
                nc.scalar.activation(th[:, :], gap[:, :], ACT.Tanh, scale=0.5).then_inc(th_done, 1)

            def comb_copy(g):
                act.wait_ge(combT_ps, g + 1)
                nc.scalar.activation(combT[:, :], up_ps[0:KB, 1, :], ACT.Copy).then_inc(combT_sb, 1)

            def gelu(g, i):
                act.wait_ge(down_done, g * NH + i + 1)
                if i == 0:
                    act.wait_ge(const_step, CONSTS)
                if i == 1:
                    act.wait_ge(lgT_done, g + 1)
                if i >= 2:
                    act.wait_ge(h_lo_done, g * NH + i - 1)
                nc.scalar.activation(gl[:, i % 2, :], down_at(i), ACT.Gelu,
                                     bias=sm[:, O_BD + i:O_BD + i + 1]).then_inc(gelu_done, 1)

            def block_hi(g, i):
                act.wait_ge(w_split, 2 * NW)
                act.wait_ge(mult_done, g * NH + i + 1)
                nc.scalar.activation(h_hi[:, i, :], gl[:, i % 2, :], ACT.Copy).then_inc(h_hi_done, 1)

            def weight_hi(n):
                act.wait_ge(w_in[n // PER_LOAD], 16)
                hi, _ = w_parts(n)
                nc.scalar.activation(hi, w_raw[:, n, :], ACT.Copy).then_inc(w_hi, 1)

            def norm_tiles(G, slot, tiles):
                for t in tiles:
                    norm(G, slot, t)
                for t in tiles:
                    norm_hi(G, t)

            act.wait_ge(small_in, 16)
            nc.scalar.activation(th[:, 0:2], sm[:, O_GX:O_GX + 2], ACT.Tanh).then_inc(tanh_done, 1)
            nc.scalar.preload_act_table_set(LN_EXP)
            nc.scalar.activation(rate[:, :], sm[:, O_TD:O_TD + NC], ACT.Exp).then_inc(decay_step, 1)
            act.wait_ge(decay_step, 1)
            nc.scalar.activation(decay[:, :], rate[:, :], ACT.Exp, scale=-1.0).then_inc(decay_step, 1)
            act.wait_ge(u_split, 2)
            nc.scalar.activation(s_old[:, :], s_old[:, :], ACT.Exp, scale=-1.0).then_inc(scales_done, 1)
            nc.scalar.activation(s_new[:, :], s_new[:, :], ACT.Exp).then_inc(scales_done, 1)
            for t in range(NT):
                exp_k(0, 0, t)
            act.wait_ge(scales_done, 2)
            scan_copy(0, 0)
            for n in range(4):
                weight_hi(n)
            scan_copy(0, 1)
            for n in range(4, 6):
                weight_hi(n)
            scan_copy(0, 2)
            for n in range(6, 8):
                weight_hi(n)
            scan_copy(0, 3)
            first_reciprocals(0, (0, 1))
            first_reciprocals(0, (2,))
            weight_hi(8)
            first_reciprocals(0, (3,))
            for n in range(9, 2 * NW):
                weight_hi(n)
            exp_k(1, 1, 0)
            exp_k(1, 1, 1)
            norm_tiles(0, 0, (0, 1))
            norm_tiles(0, 0, (2, 3))
            exp_k(1, 1, 2)
            exp_k(1, 1, 3)

            def body(g, slot, more, ahead):
                gate_act(g)
                gelu(g, 0)
                if more:
                    scan_copy(g + 1, 0)
                comb_copy(g)
                for i in range(1, NH):
                    gelu(g, i)
                    if more and i in (1, 2, 4):
                        scan_copy(g + 1, {1: 1, 2: 2, 4: 3}[i])
                    block_hi(g, i - 1)
                block_hi(g, NH - 1)
                if more:
                    nc.scalar.preload_act_table_set(LN_EXP)
                    first_reciprocals(g + 1, range(NC))
                if ahead:
                    for t in range(NT):
                        exp_k(g + 2, (slot + 2) % XS, t)
                if more:
                    norm_tiles(g + 1, (slot + 1) % XS, range(NT))

            over_groups(act, body)

        @block.vector
        def _(dve):
            V = nc.vector

            def measure1(G, slot, pair):
                for t in (2 * pair, 2 * pair + 1):
                    dve.wait_ge(x_in[t], G * 16 + 16)
                    V.bn_stats(bn[:, t, :], xs[:, slot, t, :]).then_inc(bn1_step, 1)

            def merge1(G, pair):
                measured = early(dve, G * 2 * NT + 4 * pair + 2)
                dve.wait_ge(small_in, 16)
                dve.wait_ge(bn1_step, measured)
                for t in (2 * pair, 2 * pair + 1):
                    V.bn_aggr(mv1[:, t, :], bn[:, t, :]).then_inc(bn1_step, 1)
                dve.wait_ge(bn1_step, G * 2 * NT + 4 * pair + 4)
                at = slice(2 * pair, 2 * pair + 2)
                V.tensor_scalar(ve1[:, at], mv1[:, at, 1], EPS, None, ALU.add).then_inc(ve1_done, 1)

            def shift1(G, pair):
                dve.wait_ge(rs1_done, 2 * G + pair + 1)
                dve.wait_ge(p_done, G * NT)
                at = slice(2 * pair, 2 * pair + 2)
                V.scalar_tensor_tensor(nm1[:, at], mv1[:, at, 0], -1.0, rs1[:, at], ALU.mult,
                                       ALU.mult).then_inc(nm1_done, 1)

            def scan(G, c):
                dve.wait_ge(sc_done, G * NC + c + 1)
                V.tensor_copy(nd[:, c, :, :, 0:1], nd[:, c, :, :, 1:2]).then_inc(scan_done, 1)
                dve.wait_ge(scan_done, G * 5 * NC + 5 * c + 1)
                for k in range(2):
                    for s in range(SEQS):
                        V.tensor_tensor_scan(nd[:, c, k, s, 1:SLOT], decay[:, c:c + 1].to_broadcast([P, T]),
                                             nd[:, c, k, s, 1:SLOT], 0.0, ALU.mult, ALU.add).then_inc(scan_done, 1)
                dve.wait_ge(scan_done, G * 5 * NC + 5 * (c + 1))
                pair = 2 * (c % 2)
                V.scalar_tensor_tensor(nd[:, c, :, :, 0:T],
                                       work_ps[:, pair:pair + 2, :].rearrange("p k (s t) -> p k s t", s=SEQS),
                                       s_new[:, c:c + 1], nd[:, c, :, :, 0:T], ALU.mult,
                                       ALU.add).then_inc(nd_done, 1)

            def quotient(G, c):
                dve.wait_ge(dr_done, G * NC + c + 1)
                V.scalar_tensor_tensor(halves(recip[:, c, :]), nd[:, c, 1, :, 0:T], 2.0, halves(recip[:, c, :]),
                                       ALU.subtract, ALU.mult).then_inc(r1_done, 1)
                dve.wait_ge(r1_done, G * NC + c + 1)
                V.tensor_tensor(nd[:, c, 0, :, 0:T], nd[:, c, 0, :, 0:T], halves(recip[:, c, :]),
                                ALU.mult).then_inc(y_done, 1)

            def residual(G, slot, pair):
                for t in (2 * pair, 2 * pair + 1):
                    dve.wait_ge(yT_done, G * NT + t + 1)
                    V.scalar_tensor_tensor(xs[:, slot, t, :], work_ps[:, t, :], tg[:, 0:1], xs[:, slot, t, :],
                                           ALU.mult, ALU.add).then_inc(x1_done, 1)

            def stats2(G, slot, pair):
                for t in (2 * pair, 2 * pair + 1):
                    dve.wait_ge(x1_done, G * NT + t + 1)
                    V.bn_stats(bn2[:, t, :], xs[:, slot, t, :]).then_inc(bn2_step, 1)
                measured = early(dve, G * 2 * NT + 4 * pair + 2)
                dve.wait_ge(small_in, 16)
                dve.wait_ge(bn2_step, measured)
                for t in (2 * pair, 2 * pair + 1):
                    V.bn_aggr(mv2[:, t, :], bn2[:, t, :]).then_inc(bn2_step, 1)
                dve.wait_ge(bn2_step, G * 2 * NT + 4 * pair + 4)
                at = slice(2 * pair, 2 * pair + 2)
                V.tensor_scalar(ve2[:, at], mv2[:, at, 1], EPS, None, ALU.add).then_inc(ve2_done, 1)

            def shift2(G, pair):
                dve.wait_ge(rs2_done, 2 * G + pair + 1)
                dve.wait_ge(hn_done, G * NT)
                at = slice(2 * pair, 2 * pair + 2)
                V.scalar_tensor_tensor(nm2[:, at], mv2[:, at, 0], -1.0, rs2[:, at], ALU.mult,
                                       ALU.mult).then_inc(nm2_done, 1)

            def norm_lo(G, t):
                dve.wait_ge(n_hi_done, G * NT + t + 1)
                cols = slice(t * P, (t + 1) * P)
                V.tensor_tensor(n_lo[:, :, cols], work_ps[:, t, :].rearrange("p (c n) -> p c n", c=NC),
                                n_hi[:, :, cols].bitcast(F32), ALU.subtract).then_inc(n_lo_done, 1)

            def routing(G):
                base = G * GS
                dve.wait_ge(lgT_done, G + 1)
                V.tensor_reduce(lg[:, :, :], work_ps[:, 3, 0:NT * 2 * NE]
                                .rearrange("p (t k e) -> p t e k", t=NT, k=2), AX.X, ALU.add).then_inc(gate_step, 1)
                summed = early(dve, base + 1)
                dve.wait_ge(small_in, 16)
                dve.wait_ge(gate_step, summed)
                for t in range(NT):
                    V.max(top[:, t, :], lg[:, t, :]).then_inc(gate_step, 1)
                dve.wait_ge(gate_step, base + 5)
                V.tensor_tensor(gap[:, :], top[:, :, 0], top[:, :, 1], ALU.subtract).then_inc(gate_step, 1)
                for t in range(NT):
                    V.max_index(topi[:, t, :], top[:, t, :], lg[:, t, :]).then_inc(gate_step, 1)
                dve.wait_ge(gate_step, base + 10)
                for k in range(2):
                    V.tensor_tensor(oh[:, k, :, :],
                                    sm[:, O_IOTA:O_IOTA + NE].unsqueeze(1).to_broadcast([P, NT, NE]),
                                    topi[:, :, k:k + 1].to_broadcast([P, NT, NE]), ALU.is_equal) \
                        .then_inc(gate_step, 1)
                dve.wait_ge(th_done, G + 1)
                V.tensor_scalar(wt[:, 0, :], th[:, :], tg[:, 2:3], tg[:, 2:3], ALU.mult, ALU.add) \
                    .then_inc(gate_step, 1)
                V.tensor_scalar(wt[:, 1, :], th[:, :], tg[:, 3:4], tg[:, 2:3], ALU.mult, ALU.add) \
                    .then_inc(gate_step, 1)
                dve.wait_ge(gate_step, base + 14)
                for k in range(2):
                    V.tensor_tensor(oh[:, k, :, :], oh[:, k, :, :],
                                    wt[:, k, :].unsqueeze(2).to_broadcast([P, NT, NE]), ALU.mult) \
                        .then_inc(gate_step, 1)
                dve.wait_ge(gate_step, base + 16)
                V.tensor_tensor(lg[:, :, :], oh[:, 0, :, :], oh[:, 1, :, :], ALU.add).then_inc(gate_step, 1)
                dve.wait_ge(gate_step, base + 17)
                dve.wait_ge(combT_ps, G)
                V.tensor_copy(comb[:, :, 0:NE], lg[:, :, :]).then_inc(gate_step, 1)
                V.tensor_copy(comb[:, :, 2 * NE:3 * NE], lg[:, :, :]).then_inc(gate_step, 1)
                dve.wait_ge(gate_step, base + 18)
                V.tensor_tensor(comb[:, :, NE:2 * NE], lg[:, :, :], comb[:, :, 0:NE].bitcast(F32),
                                ALU.subtract).then_inc(gate_step, 1)

            def mult(g, i):
                dve.wait_ge(gelu_done, g * NH + i + 1)
                if i == 0:
                    V.tensor_scalar(gl[:, 0, :], gl[:, 0, :], tg[:, 1:2], None, ALU.mult).then_inc(mult_done, 1)
                else:
                    dve.wait_ge(cb_done, g * NE + i)
                    V.tensor_tensor(gl[:, i % 2, :], up_ps[:, (i + 1) % 2, :], gl[:, i % 2, :],
                                    ALU.mult).then_inc(mult_done, 1)

            def finish(g, slot, t):
                dve.wait_ge(up_done, g * NT + t + 1)
                V.tensor_tensor(xs[:, slot, t, :], up_ps[:, t % 2, :], xs[:, slot, t, :],
                                ALU.add).then_inc(fin_done, 1)

            V.memset(mhalf[:, :], -0.5).then_inc(const_step, 1)
            for pair in range(2):
                measure1(0, 0, pair)
                merge1(0, pair)
            dve.wait_ge(small_in, 16)
            V.tensor_scalar(s_old[:, :], sm[:, O_TF:O_TF + NC], 0.0, None, ALU.max).then_inc(u_split, 1)
            V.tensor_scalar(s_new[:, :], sm[:, O_TF:O_TF + NC], 0.0, None, ALU.min).then_inc(u_split, 1)
            shift1(0, 0)
            shift1(0, 1)
            for t in range(NT):
                dve.wait_ge(p_done, t + 1)
                dve.wait_ge(ctx_in[t], 16)
                V.tensor_tensor(cv[:, t, :], cv[:, t, :], pk[:, t, :], ALU.mult).then_inc(pv_done, 1)
            dve.wait_ge(tanh_done, 1)
            for k, (col, f) in enumerate(((0, -1.0), (1, 1.0), (1, 0.5), (1, -0.5))):
                V.tensor_scalar(tg[:, k:k + 1], th[:, col:col + 1], f, None, ALU.mult).then_inc(tg_done, 1)
            dve.wait_ge(tg_done, 4)
            for col in (3 * NE, 3 * NE + 2):
                V.tensor_copy(comb[:, :, col], tg[:, 1:2].to_broadcast([P, NT])).then_inc(const_step, 1)
            dve.wait_ge(const_step, 3)
            V.tensor_tensor(comb[:, :, 3 * NE + 1], tg[:, 1:2].to_broadcast([P, NT]),
                            comb[:, :, 3 * NE].bitcast(F32), ALU.subtract).then_inc(const_step, 1)
            V.tensor_copy(sel[:, :], sm[0:KB, O_SEL:O_SEL + NE]).then_inc(const_step, 1)
            gate_w = sm[:, O_GW:O_GW + NC * NE].rearrange("p (c e) -> p c e", c=NC)
            gate_parts = wd_hi[:, 0:GATE].rearrange("p (c k e) -> p c k e", c=NC, k=2)
            V.tensor_copy(gate_parts[:, :, 0, :], gate_w).then_inc(const_step, 1)
            dve.wait_ge(const_step, 6)
            V.tensor_tensor(gate_parts[:, :, 1, :], gate_w, gate_parts[:, :, 0, :].bitcast(F32),
                            ALU.subtract).then_inc(const_step, 1)
            dve.wait_ge(decay_step, 2)
            dve.wait_ge(scales_done, 2)
            for c in range(NC):
                scan(0, c)
            for c in range(NC):
                quotient(0, c)
            measure1(1, 1, 0)
            merge1(1, 0)
            residual(0, 0, 0)
            shift1(1, 0)
            stats2(0, 0, 0)
            residual(0, 0, 1)
            shift2(0, 0)
            stats2(0, 0, 1)
            shift2(0, 1)
            for t in range(NT // 2):
                norm_lo(0, t)
            measure1(1, 1, 1)
            merge1(1, 1)
            for t in range(NT // 2, NT):
                norm_lo(0, t)
            shift1(1, 1)
            for t in range(2):
                dve.wait_ge(p_done, NT + t + 1)
                dve.wait_ge(ctx_in[t], 32)
                V.tensor_tensor(cv[:, t, :], cv[:, t, :], pk[:, t, :], ALU.mult).then_inc(pv_done, 1)
            dve.wait_ge(bias_in, 16)
            V.tensor_copy(bias_r[:, :], bias_raw).then_inc(const_step, 1)
            dve.wait_ge(const_step, 8)
            V.tensor_scalar(bias_raw, bias_raw, sm[0:KB, O_LOROW:O_LOROW + 1], None, ALU.mult) \
                .then_inc(const_step, 1)
            dve.wait_ge(const_step, 9)
            V.scalar_tensor_tensor(bias_r[:, :], bias_r[:, :].bitcast(F32), sm[0:KB, O_HISIGN:O_HISIGN + 1],
                                   bias_raw, ALU.mult, ALU.add).then_inc(const_step, 1)

            def body(g, slot, more, ahead):
                G, slot1 = g + 1, (slot + 1) % XS
                routing(g)
                mult(g, 0)
                for i in range(1, NH):
                    if more and i in (1, 2, 3, 5):
                        scan(G, {1: 0, 2: 1, 3: 2, 5: 3}[i])
                    mult(g, i)
                    if ahead and i == 3:
                        for pair in range(2):
                            measure1(g + 2, (slot + 2) % XS, pair)
                            merge1(g + 2, pair)
                    if ahead and i == 5:
                        shift1(g + 2, 0)
                        shift1(g + 2, 1)
                finish(g, slot, 0)
                if more:
                    for c in range(NC):
                        quotient(G, c)
                    residual(G, slot1, 0)
                finish(g, slot, 1)
                if more:
                    stats2(G, slot1, 0)
                    residual(G, slot1, 1)
                    shift2(G, 0)
                    stats2(G, slot1, 1)
                    shift2(G, 1)
                finish(g, slot, 2)
                if more:
                    for t in range(NT):
                        norm_lo(G, t)
                finish(g, slot, 3)

            over_groups(dve, body)

        @block.gpsimd
        def _(pool):
            Q = nc.gpsimd

            def rstd1(G, pair):
                pool.wait_ge(ve1_done, 2 * G + pair + 1)
                pool.wait_ge(p_done, G * NT)
                at = slice(2 * pair, 2 * pair + 2)
                Q.tensor_tensor(rs1[:, at], ve1[:, at], mhalf[:, at], ALU.pow).then_inc(rs1_done, 1)

            def rstd2(G, pair):
                pool.wait_ge(ve2_done, 2 * G + pair + 1)
                pool.wait_ge(hn_done, G * NT)
                at = slice(2 * pair, 2 * pair + 2)
                Q.tensor_tensor(rs2[:, at], ve2[:, at], mhalf[:, at], ALU.pow).then_inc(rs2_done, 1)

            def weigh_ctx(G, t):
                pool.wait_ge(p_done, G * NT + t + 1)
                pool.wait_ge(ctx_in[t], G * 16 + 16)
                Q.tensor_tensor(cv[:, t, :], cv[:, t, :], pk[:, t, :], ALU.mult).then_inc(pv_done, 1)

            def den_times_recip(G, c):
                pool.wait_ge(r0_done, G * NC + c + 1)
                Q.tensor_tensor(nd[:, c, 1, :, 0:T], nd[:, c, 1, :, 0:T], halves(recip[:, c, :]),
                                ALU.mult).then_inc(dr_done, 1)

            def block_lo(g, i):
                pool.wait_ge(h_hi_done, g * NH + i + 1)
                Q.tensor_tensor(h_lo[:, i, :], gl[:, i % 2, :], h_hi[:, i, :].bitcast(F32),
                                ALU.subtract).then_inc(h_lo_done, 1)

            def weight_lo(n):
                pool.wait_ge(w_hi, n + 1)
                hi, lo = w_parts(n)
                Q.tensor_tensor(lo, w_raw[:, n, :], hi.bitcast(F32), ALU.subtract).then_inc(w_split, 1)

            pool.wait_ge(const_step, 1)
            rstd1(0, 0)
            rstd1(0, 1)
            for n in range(8):
                weight_lo(n)
            for c in range(NC):
                den_times_recip(0, c)
            for n in range(8, 10):
                weight_lo(n)
            rstd1(1, 0)
            for n in range(10, 12):
                weight_lo(n)
            rstd2(0, 0)
            for n in range(12, 14):
                weight_lo(n)
            rstd2(0, 1)
            for n in range(14, 2 * NW - 1):
                weight_lo(n)
            rstd1(1, 1)
            weight_lo(2 * NW - 1)
            weigh_ctx(1, 2)
            weigh_ctx(1, 3)

            def body(g, slot, more, ahead):
                for i in range(NH):
                    block_lo(g, i)
                    if i == 4 and ahead:
                        rstd1(g + 2, 0)
                        rstd1(g + 2, 1)
                if more:
                    for c in range(NC):
                        den_times_recip(g + 1, c)
                    if ahead:
                        weigh_ctx(g + 2, 0)
                        weigh_ctx(g + 2, 1)
                    rstd2(g + 1, 0)
                    rstd2(g + 1, 1)
                    if ahead:
                        weigh_ctx(g + 2, 2)
                        weigh_ctx(g + 2, 3)

            over_groups(pool, body)


def kernel(x, ctx_2048, g_xattn, g_ffn, L0_xattn_time_decay, L0_xattn_time_first, L0_ffn_gate_w, L0_ffn_wd,
           L0_ffn_bd, L0_ffn_wu, L0_ffn_bu, L0_ffn_ws_d, L0_ffn_bs_d, L0_ffn_ws_u, L0_ffn_bs_u):
    import concourse.bacc as bacc
    from concourse.bass_utils import run_bass_kernel_spmd

    def a(v):
        return np.asarray(v)

    wd_all = np.concatenate([a(L0_ffn_ws_d)[None], a(L0_ffn_wd)])
    w_down = np.ascontiguousarray(wd_all.reshape(NH, BOT, NC, P).transpose(3, 0, 2, 1).reshape(P, NH * NC * BOT))
    wu_all = np.concatenate([a(L0_ffn_ws_u)[None], a(L0_ffn_wu)])
    w_up = np.ascontiguousarray(wu_all.transpose(2, 0, 1).reshape(P, NH * C))

    smalls = np.zeros((P, N_SMALL), np.float32)
    smalls[:, O_ID:O_ID + P] = np.eye(P, dtype=np.float32)
    smalls[:, O_BD:O_BD + NH] = np.concatenate([a(L0_ffn_bs_d)[None], a(L0_ffn_bd)]).T
    smalls[:, O_TD:O_TD + NC] = a(L0_xattn_time_decay).reshape(NC, P).T
    smalls[:, O_TF:O_TF + NC] = a(L0_xattn_time_first).reshape(NC, P).T
    smalls[:, O_GX:O_GX + 1] = a(g_xattn)
    smalls[:, O_GF:O_GF + 1] = a(g_ffn)
    smalls[:, O_IOTA:O_IOTA + NE] = np.arange(NE, dtype=np.float32)
    low = list(range(2 * NE, 3 * NE)) + [3 * NE + 2]
    smalls[low, O_LOROW] = 1.0
    smalls[:, O_HISIGN] = 1.0
    smalls[low, O_HISIGN] = -1.0
    for e in range(NE):
        smalls[[e, NE + e], O_SEL + e] = 1.0
    smalls[:, O_GW:] = a(L0_ffn_gate_w).reshape(NE, NC, P).transpose(2, 1, 0).reshape(P, NC * NE)
    bu, bs = a(L0_ffn_bu), a(L0_ffn_bs_u)[None]
    bias_rows = np.concatenate([bu, bu, bu, bs, bs, bs])

    nc = bacc.Bacc("TRN2", target_bir_lowering=False, num_devices=1)
    arrays = {"x": a(x).reshape(B * T, C), "ctx": a(ctx_2048).reshape(B * T, C), "smalls": smalls,
              "bias_rows": bias_rows, "w_down": w_down, "w_up": w_up}
    aps = [nc.dram_tensor(name, v.shape, mybir.dt.from_np(v.dtype), kind="ExternalInput").ap()
           for name, v in arrays.items()]
    out = nc.dram_tensor("out", (B * T, C), mybir.dt.float32, kind="ExternalOutput").ap()
    build(nc, *aps, out)
    r = run_bass_kernel_spmd(nc, [arrays], core_ids=[0])
    return r.results[0]["out"].reshape(B, T, C)
```
